# Optimizing a Trainium2 kernel written in Bass

```python
import numpy as np
import jax
import jax.numpy as jnp

def _softmax(x, axis=-1):
    return jax.nn.softmax(x, axis=axis)

def _gelu(x):
    return jax.nn.gelu(x, approximate=True)

def _silu(x):
    return jax.nn.silu(x)

def _sigmoid(x):
    return jax.nn.sigmoid(x)

def _layernorm(x, axis=-1, eps=1e-05):
    m = jnp.mean(x, axis=axis, keepdims=True)
    v = jnp.var(x, axis=axis, keepdims=True)
    return (x - m) / jnp.sqrt(v + eps)

def _scatter_add(tgt, idx, src, axis=0):
    return tgt.at[idx].add(src)

def _segment_sum(src, seg, n):
    return jax.ops.segment_sum(src, seg, n)
kernel_name = 'mk_conv_seq_d2_conv_nchw256_r2_c8f706'

def setup_inputs(seed: int=0):
    np.random.seed(seed)
    _w = jnp.asarray

    def _rec_inputs():
        import jax
        import jax.numpy as jnp
        _gk = jax.random.key(seed)
        x = -0.0002928 + 1 * jax.random.normal(jax.random.fold_in(_gk, 1), (4, 128, 32, 32), jnp.float32)
        return x
    x = _rec_inputs()

    def _L0_conv_setup():
        import jax, jax.numpy as jnp
        import numpy as np
        DY = jnp.array([-1, -1, -1, 0, 0, 0, 1, 1, 1], dtype=jnp.float32)
        DX = jnp.array([-1, 0, 1, -1, 0, 1, -1, 0, 1], dtype=jnp.float32)
        REG = jnp.stack([DY, DX])
        EPS = 1e-05

        def conv3x3(x, w, b):
            y = jax.lax.conv_general_dilated(x, w, (1, 1), ((1, 1), (1, 1)), dimension_numbers=('NCHW', 'OIHW', 'NCHW'))
            return y + b[None, :, None, None]

        def batchnorm(x, gamma, beta):
            m = x.mean((0, 2, 3), keepdims=True)
            v = x.var((0, 2, 3), keepdims=True)
            return gamma[None, :, None, None] * (x - m) * jax.lax.rsqrt(v + EPS) + beta[None, :, None, None]

        def make_offset(tm, tr):
            N, _, H, W = tm.shape
            M = tm.transpose(0, 2, 3, 1).reshape(N, H, W, 2, 2)
            off = jnp.einsum('nhwij,jk->nhwik', M, REG) - REG
            off = off.transpose(0, 4, 3, 1, 2)
            off = off + tr[:, None, :, :, :]
            return off

        def deform_conv(x, off, w):
            N, C, H, W = x.shape
            K = 9
            py = jnp.arange(H, dtype=x.dtype)[None, None, :, None] + DY[None, :, None, None] + off[:, :, 0]
            px = jnp.arange(W, dtype=x.dtype)[None, None, None, :] + DX[None, :, None, None] + off[:, :, 1]
            y0 = jnp.floor(py)
            x0 = jnp.floor(px)
            wy = py - y0
            wx = px - x0
            y0i = y0.astype(jnp.int32)
            x0i = x0.astype(jnp.int32)
            x_flat = x.reshape(N, C, H * W)

            def corner(yi, xi, wgt):
                valid = (yi >= 0) & (yi < H) & (xi >= 0) & (xi < W)
                idx = jnp.clip(yi, 0, H - 1) * W + jnp.clip(xi, 0, W - 1)
                g = jax.vmap(lambda xf, ix: xf[:, ix])(x_flat, idx.reshape(N, -1))
                g = g.reshape(N, C, K, H, W)
                return g * (wgt * valid)[:, None]
            cols = corner(y0i, x0i, (1 - wy) * (1 - wx)) + corner(y0i, x0i + 1, (1 - wy) * wx) + corner(y0i + 1, x0i, wy * (1 - wx)) + corner(y0i + 1, x0i + 1, wy * wx)
            Co = w.shape[0]
            return jnp.einsum('nckhw,ock->nohw', cols, w.reshape(Co, C, K))
        key = jax.random.key(seed)
        ks = jax.random.split(key, 16)
        N, C, Co, H, W = (4, 128, 128, 32, 32)
        s_off = 0.02
        s_w = 0.05
        return {'x': jax.random.normal(ks[0], (N, C, H, W), jnp.float32), 'tm1_w': jax.random.normal(ks[1], (4, C, 3, 3), jnp.float32) * s_off, 'tm1_b': jax.random.normal(ks[2], (4,), jnp.float32) * s_off, 'tr1_w': jax.random.normal(ks[3], (2, C, 3, 3), jnp.float32) * s_off, 'tr1_b': jax.random.normal(ks[4], (2,), jnp.float32) * s_off, 'dcn1_w': jax.random.normal(ks[5], (Co, C, 3, 3), jnp.float32) * s_w, 'bn1_g': jnp.ones((Co,), jnp.float32), 'bn1_b': jnp.zeros((Co,), jnp.float32), 'tm2_w': jax.random.normal(ks[6], (4, Co, 3, 3), jnp.float32) * s_off, 'tm2_b': jax.random.normal(ks[7], (4,), jnp.float32) * s_off, 'tr2_w': jax.random.normal(ks[8], (2, Co, 3, 3), jnp.float32) * s_off, 'tr2_b': jax.random.normal(ks[9], (2,), jnp.float32) * s_off, 'dcn2_w': jax.random.normal(ks[10], (Co, Co, 3, 3), jnp.float32) * s_w, 'bn2_g': jnp.ones((Co,), jnp.float32), 'bn2_b': jnp.zeros((Co,), jnp.float32)}
    _L0_conv_all = _L0_conv_setup()
    _L0_conv_in = {k: v for k, v in _L0_conv_all.items() if k in ('tm1_w', 'tm1_b', 'tr1_w', 'tr1_b', 'dcn1_w', 'bn1_g', 'bn1_b', 'tm2_w', 'tm2_b', 'tr2_w', 'tr2_b', 'dcn2_w', 'bn2_g', 'bn2_b')}
    del _L0_conv_all

    def _L1_conv_setup():
        import jax, jax.numpy as jnp
        import numpy as np
        B, C, H, W = (8, 128, 32, 32)
        C8 = C // 8
        key = jax.random.key(seed)
        ks = jax.random.split(key, 8)
        s = 0.02
        return {'x': jax.random.normal(ks[0], (B, C, H, W), dtype=jnp.float32), 'wq': jax.random.normal(ks[1], (C8, C), dtype=jnp.float32) * s, 'bq': jnp.zeros((C8,), dtype=jnp.float32), 'wk': jax.random.normal(ks[2], (C8, C), dtype=jnp.float32) * s, 'bk': jnp.zeros((C8,), dtype=jnp.float32), 'wv': jax.random.normal(ks[3], (C, C), dtype=jnp.float32) * s, 'bv': jnp.zeros((C,), dtype=jnp.float32), 'gamma': jnp.float32(0.5)}
    _L1_conv_all = _L1_conv_setup()
    _L1_conv_in = {k: v for k, v in _L1_conv_all.items() if k in ('wq', 'bq', 'wk', 'bk', 'wv', 'bv', 'gamma')}
    del _L1_conv_all
    return {'x': x, 'L0_conv_tm1_w': _L0_conv_in['tm1_w'], 'L0_conv_tm1_b': _L0_conv_in['tm1_b'], 'L0_conv_tr1_w': _L0_conv_in['tr1_w'], 'L0_conv_tr1_b': _L0_conv_in['tr1_b'], 'L0_conv_dcn1_w': _L0_conv_in['dcn1_w'], 'L0_conv_bn1_g': _L0_conv_in['bn1_g'], 'L0_conv_bn1_b': _L0_conv_in['bn1_b'], 'L0_conv_tm2_w': _L0_conv_in['tm2_w'], 'L0_conv_tm2_b': _L0_conv_in['tm2_b'], 'L0_conv_tr2_w': _L0_conv_in['tr2_w'], 'L0_conv_tr2_b': _L0_conv_in['tr2_b'], 'L0_conv_dcn2_w': _L0_conv_in['dcn2_w'], 'L0_conv_bn2_g': _L0_conv_in['bn2_g'], 'L0_conv_bn2_b': _L0_conv_in['bn2_b'], 'L1_conv_wq': _L1_conv_in['wq'], 'L1_conv_bq': _L1_conv_in['bq'], 'L1_conv_wk': _L1_conv_in['wk'], 'L1_conv_bk': _L1_conv_in['bk'], 'L1_conv_wv': _L1_conv_in['wv'], 'L1_conv_bv': _L1_conv_in['bv'], 'L1_conv_gamma': _L1_conv_in['gamma']}

def reference(x, L0_conv_tm1_w, L0_conv_tm1_b, L0_conv_tr1_w, L0_conv_tr1_b, L0_conv_dcn1_w, L0_conv_bn1_g, L0_conv_bn1_b, L0_conv_tm2_w, L0_conv_tm2_b, L0_conv_tr2_w, L0_conv_tr2_b, L0_conv_dcn2_w, L0_conv_bn2_g, L0_conv_bn2_b, L1_conv_wq, L1_conv_bq, L1_conv_wk, L1_conv_bk, L1_conv_wv, L1_conv_bv, L1_conv_gamma):
    import jax
    import jax.numpy as jnp

    def _L0_conv_ref(x, tm1_w, tm1_b, tr1_w, tr1_b, dcn1_w, bn1_g, bn1_b, tm2_w, tm2_b, tr2_w, tr2_b, dcn2_w, bn2_g, bn2_b):
        import jax, jax.numpy as jnp
        import numpy as np
        DY = jnp.array([-1, -1, -1, 0, 0, 0, 1, 1, 1], dtype=jnp.float32)
        DX = jnp.array([-1, 0, 1, -1, 0, 1, -1, 0, 1], dtype=jnp.float32)
        REG = jnp.stack([DY, DX])
        EPS = 1e-05

        def conv3x3(x, w, b):
            y = jax.lax.conv_general_dilated(x, w, (1, 1), ((1, 1), (1, 1)), dimension_numbers=('NCHW', 'OIHW', 'NCHW'))
            return y + b[None, :, None, None]

        def batchnorm(x, gamma, beta):
            m = x.mean((0, 2, 3), keepdims=True)
            v = x.var((0, 2, 3), keepdims=True)
            return gamma[None, :, None, None] * (x - m) * jax.lax.rsqrt(v + EPS) + beta[None, :, None, None]

        def make_offset(tm, tr):
            N, _, H, W = tm.shape
            M = tm.transpose(0, 2, 3, 1).reshape(N, H, W, 2, 2)
            off = jnp.einsum('nhwij,jk->nhwik', M, REG) - REG
            off = off.transpose(0, 4, 3, 1, 2)
            off = off + tr[:, None, :, :, :]
            return off

        def deform_conv(x, off, w):
            N, C, H, W = x.shape
            K = 9
            py = jnp.arange(H, dtype=x.dtype)[None, None, :, None] + DY[None, :, None, None] + off[:, :, 0]
            px = jnp.arange(W, dtype=x.dtype)[None, None, None, :] + DX[None, :, None, None] + off[:, :, 1]
            y0 = jnp.floor(py)
            x0 = jnp.floor(px)
            wy = py - y0
            wx = px - x0
            y0i = y0.astype(jnp.int32)
            x0i = x0.astype(jnp.int32)
            x_flat = x.reshape(N, C, H * W)

            def corner(yi, xi, wgt):
                valid = (yi >= 0) & (yi < H) & (xi >= 0) & (xi < W)
                idx = jnp.clip(yi, 0, H - 1) * W + jnp.clip(xi, 0, W - 1)
                g = jax.vmap(lambda xf, ix: xf[:, ix])(x_flat, idx.reshape(N, -1))
                g = g.reshape(N, C, K, H, W)
                return g * (wgt * valid)[:, None]
            cols = corner(y0i, x0i, (1 - wy) * (1 - wx)) + corner(y0i, x0i + 1, (1 - wy) * wx) + corner(y0i + 1, x0i, wy * (1 - wx)) + corner(y0i + 1, x0i + 1, wy * wx)
            Co = w.shape[0]
            return jnp.einsum('nckhw,ock->nohw', cols, w.reshape(Co, C, K))
        residual = x
        off1 = make_offset(conv3x3(x, tm1_w, tm1_b), conv3x3(x, tr1_w, tr1_b))
        out = deform_conv(x, off1, dcn1_w)
        out = jax.nn.relu(batchnorm(out, bn1_g, bn1_b))
        off2 = make_offset(conv3x3(out, tm2_w, tm2_b), conv3x3(out, tr2_w, tr2_b))
        out = deform_conv(out, off2, dcn2_w)
        out = batchnorm(out, bn2_g, bn2_b)
        return jax.nn.relu(out + residual)

    def _L1_conv_ref(x, wq, bq, wk, bk, wv, bv, gamma):
        import jax, jax.numpy as jnp
        import numpy as np
        B, C, H, W = (8, 128, 32, 32)
        C8 = C // 8
        b, c, h, w = x.shape
        f = x.reshape(b, c, h * w)
        q = jnp.einsum('oc,bcn->bno', wq, f) + bq
        k = jnp.einsum('oc,bcn->bon', wk, f) + bk[None, :, None]
        v = jnp.einsum('oc,bcn->bon', wv, f) + bv[None, :, None]
        scores = jnp.einsum('bnc,bcm->bnm', q, k)
        attn = jax.nn.softmax(scores, axis=1)
        out = jnp.einsum('bcn,bnm->bcm', v, attn)
        out = out.reshape(b, c, h, w)
        return gamma * out + x

    def _gn(v, G=32, eps=1e-05):
        B_, C_, H_, W_ = v.shape
        g = v.reshape(B_, G, C_ // G, H_, W_)
        m = jnp.mean(g, axis=(2, 3, 4), keepdims=True)
        s = jnp.var(g, axis=(2, 3, 4), keepdims=True)
        return ((g - m) / jnp.sqrt(s + eps)).reshape(v.shape)

    def _ln_c(v, eps=1e-06):
        m = jnp.mean(v, axis=1, keepdims=True)
        s = jnp.var(v, axis=1, keepdims=True)
        return (v - m) / jnp.sqrt(s + eps)

    def _ln_t(v, eps=1e-05):
        m = jnp.mean(v, axis=-1, keepdims=True)
        s = jnp.var(v, axis=-1, keepdims=True)
        return (v - m) / jnp.sqrt(s + eps)

    def _to_tokens(v):
        B_, C_, H_, W_ = v.shape
        return v.reshape(B_, C_, H_ * W_).transpose(0, 2, 1)

    def _from_tokens(t, like):
        B_, C_, H_, W_ = like.shape
        return t.transpose(0, 2, 1).reshape(B_, C_, H_, W_)
    x = _L0_conv_ref(x, L0_conv_tm1_w, L0_conv_tm1_b, L0_conv_tr1_w, L0_conv_tr1_b, L0_conv_dcn1_w, L0_conv_bn1_g, L0_conv_bn1_b, L0_conv_tm2_w, L0_conv_tm2_b, L0_conv_tr2_w, L0_conv_tr2_b, L0_conv_dcn2_w, L0_conv_bn2_g, L0_conv_bn2_b)
    x = _L1_conv_ref(x, L1_conv_wq, L1_conv_bq, L1_conv_wk, L1_conv_bk, L1_conv_wv, L1_conv_bv, L1_conv_gamma)
    return x

_drawn_inputs = setup_inputs


def setup_inputs(seed=0):
    import zlib

    import numpy as np

    out = dict(_drawn_inputs(seed))
    spreads = {'L0_conv_bn1_g': (1.0, 0.2),
     'L0_conv_bn1_b': (0.0, 0.1),
     'L0_conv_bn2_g': (1.0, 0.2),
     'L0_conv_bn2_b': (0.0, 0.1),
     'L1_conv_bq': (0.0, 0.8),
     'L1_conv_bk': (0.0, 0.8),
     'L1_conv_bv': (0.0, 0.1)}
    factors = {'L0_conv_tr2_b': 6.864, 'L1_conv_wq': 8.0, 'L1_conv_wk': 8.0}
    for name, (base, spread) in spreads.items():
        noise = np.random.default_rng([zlib.crc32(name.encode()), seed]).standard_normal(out[name].shape)
        drawn = base * np.exp(spread * noise) if base else spread * noise
        out[name] = jnp.asarray(drawn.astype(out[name].dtype))
    for name, factor in factors.items():
        out[name] = (out[name] * factor).astype(out[name].dtype)
    return out
```

```python
import concourse.bass as bass
from concourse import mybir
from contextlib import ExitStack


def deform_resblock_attention(nc, x, tm_w, tm_b, tr_w, tr_b, dcn_w, bn_g, bn_b,
                              wq, bq, wk, bk, wv, bv, gamma, out, table):
    f32, i32 = mybir.dt.float32, mybir.dt.int32
    ALU, ACT, AX = mybir.AluOpType, mybir.ActivationFunctionType, mybir.AxisListType
    ds = bass.ds

    N, C, H, W = x.shape
    HW = H * W
    PIX = N * HW
    P = 128
    assert N * W == P and C == P
    KH = 3
    TAPS = KH * KH
    NOFF = 6
    ROWS = 4
    GROUPS = H // ROWS
    GT = TAPS * ROWS
    TILES = GROUPS * GT
    GCOL = ROWS * P
    BANK = 512
    CORNERS = [(0, 0), (0, 1), (1, 0), (1, 1)]
    TS = HW // P
    UNITS = 3
    BODY = 2
    ROUND = 12582912.0
    BN_EPS = 1e-5
    D = wq.shape[0]
    LAYERS = 2
    BIAS = [0, NOFF]
    BV = LAYERS * NOFF
    GAM = BV + C
    ROWLEN = GAM + 1

    with ExitStack() as ctx:
        def sb(name, shape, dt=f32):
            return ctx.enter_context(nc.sbuf_tensor(name, shape, dt))

        def sem(name):
            return ctx.enter_context(nc.semaphore(name))

        X = sb("X", [P, PIX])
        A = [sb(f"A{l}", [P, PIX]) for l in range(LAYERS)]
        XH = sb("XH", [P, PIX])
        XN = [X, A[1]]
        XT = sb("XT", [P, PIX // P, C])
        ZS = sb("ZS", [P, H, TAPS * NOFF])
        OFF = sb("OFF", [P, H, NOFF])
        shift = sb("shift", [P, KH, P])
        ident = shift[:, 1, :]
        zeros = sb("zeros", [W + 1, C])
        ones = sb("ones", [1, P])
        grid_i = sb("grid_i", [P, 2 + H], i32)
        gridw = sb("gridw", [P, 1])
        gridn = sb("gridn", [P, 1])
        gridh = sb("gridh", [P, H])
        base = sb("base", [P, 2, H])
        rowpos = sb("rowpos", [P, 2, KH, H])
        pos = sb("pos", [P, 2, TILES])
        low = sb("low", [P, 2, TILES])
        dist = sb("dist", [P, 2, TILES])
        hat = sb("hat", [P, 2, 2, TILES])
        hat_t = sb("hat_t", [P, 2, TILES])
        wgt = sb("wgt", [P, TILES, 4])
        rowf = sb("rowf", [P, TILES])
        rowi = sb("rowi", [P, TILES], i32)
        rows_now = sb("rows_now", [P, BODY, GT], i32)
        G = sb("G", [P, UNITS, ROWS, 4 * C])
        V = sb("V", [P, 2, ROWS, C])
        CT = sb("CT", [P, 2, GCOL])
        dcn_nat = [sb(f"dcn_nat{l}", [P, C * TAPS]) for l in range(LAYERS)]
        dcn_T = [sb(f"dcn_T{l}", [P, TAPS, P]) for l in range(LAYERS)]
        off_nat = [sb(f"off_nat{l}", [NOFF, C * TAPS]) for l in range(LAYERS)]
        off_T = [sb(f"off_T{l}", [P, TAPS * NOFF]) for l in range(LAYERS)]
        row = sb("row", [1, ROWLEN])
        rowb = sb("rowb", [P, ROWLEN])
        bn = [sb(f"bn{l}", [P, 2]) for l in range(LAYERS)]
        stats = sb("stats", [P, GROUPS, 6])
        mv = sb("mv", [P, 2])
        nrm = sb("nrm", [P, 8])
        veps = nrm[:, 0:1]
        root = nrm[:, 1:2]
        rinv = nrm[:, 2:3]
        sq = nrm[:, 3:4]
        corr = nrm[:, 4:5]
        bn_scale = nrm[:, 5:6]
        mscale = nrm[:, 6:7]
        bn_shift = nrm[:, 7:8]
        qkv_nat = sb("qkv_nat", [P, 3, C])
        qk_T = sb("qk_T", [P, 64])
        wv_T = sb("wv_T", [P, C])
        qk_b = sb("qk_b", [D, 2])
        F = sb("F", [P, HW])
        qk = sb("qk", [D, 2, HW])
        vT = sb("vT", [P, TS, C])
        probT = XT[:, 0:2 * TS, :].rearrange("p (b t) k -> p b (t k)", b=2)
        prob = XT[:, 2 * TS:4 * TS, :].rearrange("p (b t) k -> p b t k", b=2)
        nmax = sb("nmax", [P, 2])
        esum = sb("esum", [P, 4])
        einv = sb("einv", [P, 2])
        yT = sb("yT", [P, 2, C])
        OUT = sb("OUT", [P, 2, 4 * P])

        bank = [ctx.enter_context(nc.psum_tensor(f"bank{i}", [P, BANK], f32)) for i in range(4)]
        pair = [ctx.enter_context(nc.psum_tensor(f"pair{i}", [P, 2 * BANK], f32)) for i in range(2)]
        conv_acc = pair[0][:, 0:BANK]
        off_acc = pair[0][:, BANK:BANK + H * NOFF]

        x_in = [sem(f"x_in{n}") for n in range(N)]
        offw_in = sem("offw_in")
        dcnw_in = sem("dcnw_in")
        small_in = sem("small_in")
        consts = sem("consts")
        consts_dve = sem("consts_dve")
        wgt_ready = sem("wgt_ready")
        einv_ready = sem("einv_ready")
        fill_out = sem("fill_out")
        setup_pe = sem("setup_pe")
        setup_cp = sem("setup_cp")
        xt_pe = sem("xt_pe")
        xt_dve = sem("xt_dve")
        xt_act = sem("xt_act")
        z_pe = sem("z_pe")
        z_act = sem("z_act")
        off_pe = sem("off_pe")
        dve_step = sem("dve_step")
        rows_ready = sem("rows_ready")
        table_out = [sem(f"table_out{l}") for l in range(LAYERS)]
        rows_copied = sem("rows_copied")
        gathered = [[sem(f"gathered{l}_{u}") for u in range(UNITS)] for l in range(LAYERS)]
        scaled = [sem(f"scaled{l}") for l in range(LAYERS)]
        corner = [sem(f"corner{l}") for l in range(LAYERS)]
        blended = [sem(f"blended{l}") for l in range(LAYERS)]
        turned = [sem(f"turned{l}") for l in range(LAYERS)]
        turned_cp = [sem(f"turned_cp{l}") for l in range(LAYERS)]
        conv_mm = [sem(f"conv_mm{l}") for l in range(LAYERS)]
        acc_cp = [sem(f"acc_cp{l}") for l in range(LAYERS)]
        acc_stats = [sem(f"acc_stats{l}") for l in range(LAYERS)]
        var_ready = sem("var_ready")
        root_ready = sem("root_ready")
        norm_ready = sem("norm_ready")
        xh_ready = sem("xh_ready")
        bn_done = sem("bn_done")
        res_add = sem("res_add")
        f_ready = sem("f_ready")
        qk_pe = sem("qk_pe")
        qk_cp = sem("qk_cp")
        v_pe = sem("v_pe")
        v_cp = sem("v_cp")
        score = sem("score")
        maxed = sem("maxed")
        expd = sem("expd")
        p_pe = sem("p_pe")
        p_dve = sem("p_dve")
        p_act = sem("p_act")
        o_pe = sem("o_pe")
        y_ready = sem("y_ready")
        y_pe = sem("y_pe")
        out_ready = sem("out_ready")
        out_dma = sem("out_dma")
        out_free = sem("out_free")

        G_CREDIT = UNITS
        CREDIT = 2
        P_CREDIT = 4
        Y_CREDIT = 4
        OUT_CREDIT = 1

        CONSTS = 1 + KH + 4
        SMALL = 4 * LAYERS + 7

        def by_row(t):
            return t.rearrange("c (h n w) -> c n h w", h=H, n=N)

        out_v = out.rearrange("n c h w -> c n (h w)")

        def tile_cols(l, n, t):
            return XN[l][:, n * HW + t * P:n * HW + (t + 1) * P]

        block = ctx.enter_context(nc.Block())

        @block.sync
        def _(sp):
            for n in range(N):
                sp.dma_start(X[:, n * HW:(n + 1) * HW],
                             x[n].rearrange("c h w -> c (h w)")).then_inc(x_in[n], 16)
            for l in range(LAYERS):
                sp.dma_start(dcn_nat[l][:], dcn_w[l].rearrange("o c i j -> o (c i j)")).then_inc(dcnw_in, 16)
            sp.wait_ge(consts_dve, 1)
            for s, (dy, dx) in enumerate(CORNERS):
                back = dy * W + dx
                head = W + 1 - back
                if head:
                    sp.dma_start(table[0:head, s * C:(s + 1) * C], zeros[0:head, :]).then_inc(fill_out, 16)
                if back:
                    sp.dma_start(table[PIX + head:PIX + W + 1, s * C:(s + 1) * C],
                                 zeros[0:back, :]).then_inc(fill_out, 16)
            for l in range(LAYERS):
                if l:
                    sp.wait_ge(conv_mm[l - 1], CREDIT + GROUPS * TAPS)
                for n in range(N):
                    sp.wait_ge(xt_dve, l * N + n + 1)
                    sp.wait_ge(xt_act, l * N + n + 1)
                    for s, (dy, dx) in enumerate(CORNERS):
                        first = n * HW + W + 1 - (dy * W + dx)
                        sp.dma_start(table[first:first + HW, s * C:(s + 1) * C].rearrange("(t p) c -> p t c", p=P),
                                     XT[:, n * TS:(n + 1) * TS, :]).then_inc(table_out[l], 16)
            with sp.Fori(0, N) as n:
                for half in range(2):
                    sp.wait_ge(out_ready, n * 2 + (half + 1 + OUT_CREDIT))
                    sp.dma_start(out_v[:, ds(n, 1), half * 512:(half + 1) * 512],
                                 OUT[:, half, :].unsqueeze(1)).then_inc(out_dma, 16)
                    sp.wait_ge(out_dma, n * 32 + 16 * (half + 1))
                    sp.sem_inc(out_free, 1)
            sp.wait_ge(out_dma, 16 * 2 * N)
            sp.wait_ge(fill_out, 16 * 6)

        @block.gpsimd
        def _(pool):
            pool.memset(shift[:], 0.0).then_inc(consts, 1)
            pool.wait_ge(consts, 1)
            for j in range(KH):
                pool.affine_select(out=shift[:, j, :], in_=shift[:, j, :], compare_op=ALU.not_equal, fill=1.0,
                                   base=-(j - 1), pattern=[[-1, P]], channel_multiplier=1).then_inc(consts, 1)
            pool.wait_ge(consts, 1 + KH)
            pool.memset(shift[:, 0, :].rearrange("p (n w) -> p n w", w=W)[:, :, 0:1], 0.0).then_inc(consts, 1)
            pool.memset(shift[:, 2, :].rearrange("p (n w) -> p n w", w=W)[:, :, W - 1:W], 0.0).then_inc(consts, 1)
            pool.iota(grid_i[:, 0:2], pattern=[[0, 2]], base=0, channel_multiplier=1).then_inc(consts, 1)
            pool.iota(grid_i[:, 2:2 + H], pattern=[[1, H]], base=0, channel_multiplier=0).then_inc(consts, 1)

            for n in range(N):
                pool.wait_ge(x_in[n], 16)
                pool.tensor_copy(by_row(XH[:])[:, n], X[:, n * HW:(n + 1) * HW].rearrange("c (h w) -> c h w", w=W)) \
                    .then_inc(xh_ready, 1)

            for l in range(LAYERS):
                pool.wait_ge(rows_ready, l + 1)
                pool.wait_ge(fill_out, 16 * 6)
                pool.wait_ge(table_out[l], 16 * 4 * N)
                with pool.Fori(0, GROUPS // BODY) as it:
                    for b in range(BODY):
                        pool.wait_ge(blended[l], it * (BODY * TAPS) + (b * TAPS + 1))
                        pool.tensor_copy(rows_now[:, b, :], rowi[:, ds(it * (BODY * GT) + b * GT, GT)]) \
                            .then_inc(rows_copied, 1)
                        pool.wait_ge(rows_copied, it * BODY + (l * GROUPS + b + 1))
                        pool.nop(nofuse=True)
                        for k in range(TAPS):
                            kb = b * TAPS + k
                            if k:
                                pool.wait_ge(blended[l], it * (BODY * TAPS) + (kb + 1))
                                pool.nop(nofuse=True)
                            for r in range(ROWS):
                                c = k * ROWS + r
                                pool.indirect_dma_start(
                                    G[:, kb % UNITS, r, :], None, table[:, :],
                                    bass.IndirectOffsetOnAxis(rows_now[:, b, c:c + 1], 0)) \
                                    .then_inc(gathered[l][kb % UNITS], 16)

        @block.scalar
        def _(act):
            for l in range(LAYERS):
                act.dma_start(off_nat[l][0:4, :], tm_w[l].rearrange("o c i j -> o (c i j)")).then_inc(offw_in, 16)
                act.dma_start(off_nat[l][4:6, :], tr_w[l].rearrange("o c i j -> o (c i j)")).then_inc(offw_in, 16)
                act.dma_start(row[:, BIAS[l]:BIAS[l] + 4], tm_b[l].rearrange("(a n) -> a n", a=1)).then_inc(small_in, 16)
                act.dma_start(row[:, BIAS[l] + 4:BIAS[l] + 6],
                              tr_b[l].rearrange("(a n) -> a n", a=1)).then_inc(small_in, 16)
                act.dma_start(bn[l][:, 0:1], bn_g[l].rearrange("(n a) -> n a", a=1)).then_inc(small_in, 16)
                act.dma_start(bn[l][:, 1:2], bn_b[l].rearrange("(n a) -> n a", a=1)).then_inc(small_in, 16)
            act.dma_start(row[:, BV:BV + C], bv.rearrange("(a n) -> a n", a=1)).then_inc(small_in, 16)
            act.dma_start(row[:, GAM:GAM + 1], gamma.rearrange("(a n) -> a n", a=1)).then_inc(small_in, 16)
            act.dma_start(qk_b[:, 0:1], bq.rearrange("(n a) -> n a", a=1)).then_inc(small_in, 16)
            act.dma_start(qk_b[:, 1:2], bk.rearrange("(n a) -> n a", a=1)).then_inc(small_in, 16)
            act.dma_start(qkv_nat[0:D, 0, :], wq).then_inc(small_in, 16)
            act.dma_start(qkv_nat[0:D, 1, :], wk).then_inc(small_in, 16)
            act.dma_start(qkv_nat[:, 2, :], wv).then_inc(small_in, 16)

            for l in range(LAYERS):
                for n in range(N):
                    act.wait_ge(xt_pe, l * 2 * N + 2 * n + 2)
                    if l and n == 0:
                        act.wait_ge(table_out[0], 16 * 4 * N)
                    act.copy(XT[:, n * TS + 4:(n + 1) * TS, :], bank[1][:]).then_inc(xt_act, 1)
                if l == 0:
                    act.wait_ge(setup_pe, 1)
                    for m in range(LAYERS):
                        act.copy(off_T[m][:], pair[1][:, m * TAPS * NOFF:(m + 1) * TAPS * NOFF])
                    act.copy(rowb[:], pair[1][:, 128:128 + ROWLEN])
                    act.copy(qk_T[:, 0:D], pair[1][:, 320:320 + D])
                    act.copy(qk_T[:, 32:32 + D], pair[1][:, 352:352 + D])
                    act.copy(wv_T[:], pair[1][:, 384:512]).then_inc(setup_cp, 1)
                for q in range(4):
                    act.wait_ge(z_pe, l * 4 + q + 1)
                    act.copy(ZS[:, q * 8:(q + 1) * 8, :], bank[2 + q % 2][:, 0:8 * TAPS * NOFF]).then_inc(z_act, 1)

                if l == 0:
                    for m in range(LAYERS):
                        act.wait_ge(setup_pe, 2 + m)
                        act.copy(dcn_T[m][:, 0:4, :], bank[2][:])
                        act.copy(dcn_T[m][:, 4:8, :], bank[3][:])
                        act.copy(dcn_T[m][:, 8, :], pair[1][:, 0:P]).then_inc(setup_cp, 1)
                act.wait_ge(wgt_ready, l + 1)

                def scale(it, kb):
                    act.wait_ge(gathered[l][kb % UNITS], it * (16 * ROWS * BODY * TAPS // UNITS)
                                + 16 * ROWS * (kb // UNITS + 1))
                    act.wait_ge(turned[l], it * (BODY * TAPS) + (kb + 1))
                    for r in range(ROWS):
                        last = act.activation(
                            V[:, kb % 2, r, :], G[:, kb % UNITS, r, 0:C], ACT.Copy,
                            scale=wgt[:, ds(it * (BODY * GT) + (kb * ROWS + r), 1), 0])
                    last.then_inc(scaled[l], 1)

                def turned_copy(it, kb):
                    act.wait_ge(turned[l], it * (BODY * TAPS) + (kb + 1 + CREDIT))
                    act.wait_ge(conv_mm[l], it * (BODY * TAPS) + (kb + 1))
                    act.copy(CT[:, kb % 2, :], bank[kb % 2][:]).then_inc(turned_cp[l], 1)

                with act.Fori(0, GROUPS // BODY) as it:
                    for kb in range(BODY * TAPS):
                        scale(it, kb)
                        if kb:
                            turned_copy(it, kb - 1)
                        if kb == TAPS:
                            act.wait_ge(conv_mm[l], it * (BODY * TAPS) + (TAPS + CREDIT))
                            act.copy(A[l][:, ds(it * (BODY * GCOL), GCOL)], conv_acc).then_inc(acc_cp[l], 1)
                    turned_copy(it, BODY * TAPS - 1)
                    act.wait_ge(conv_mm[l], it * (BODY * TAPS) + (BODY * TAPS + CREDIT))
                    act.copy(A[l][:, ds(it * (BODY * GCOL) + GCOL, GCOL)], conv_acc).then_inc(acc_cp[l], 1)

                act.wait_ge(var_ready, l + 1)
                act.sqrt(root, veps).then_inc(root_ready, 1)
                if l == 0:
                    act.wait_ge(norm_ready, 1)
                    act.wait_ge(acc_cp[0], GROUPS + 1)
                    for n in range(N):
                        act.activation(XN[1][:, n * HW:(n + 1) * HW].rearrange("c (h w) -> c h w", w=W),
                                       by_row(A[0][:])[:, n], ACT.Relu,
                                       bias=bn_shift, scale=bn_scale).then_inc(bn_done, 1)

            with act.Fori(0, N) as n:
                act.wait_ge(res_add, n + 1)
                act.activation(F[:], F[:], ACT.Relu, bias=bn_shift).then_inc(f_ready, 1)
                act.wait_ge(qk_pe, n + 1)
                act.activation(qk[:, 0, :], pair[0][0:D, :], ACT.Identity, bias=qk_b[:, 0:1]).then_inc(qk_cp, 1)
                act.activation(qk[:, 1, :], pair[0][32:32 + D, :], ACT.Identity,
                               bias=qk_b[:, 1:2]).then_inc(qk_cp, 1)

                def exps(t):
                    act.wait_ge(maxed, n * TS + (t + 1))
                    act.wait_ge(p_pe, n * (2 * TS) + (2 * t + 2))
                    act.wait_ge(y_ready, n * TS + (t + 1))
                    act.activation(probT[:, t % 2, :], pair[t % 2][:], ACT.Exp, bias=nmax[:, t % 2:t % 2 + 1],
                                   accum_out=esum[:, t % 4:t % 4 + 1]).then_inc(expd, 1)

                exps(0)
                exps(1)
                for t in range(TS):
                    act.wait_ge(p_pe, n * (2 * TS) + (2 * t + 2 + P_CREDIT))
                    act.wait_ge(o_pe, n * TS + (t + 1))
                    act.copy(prob[:, t % 2, 4:8, :], bank[1][:]).then_inc(p_act, 1)
                    if t + 2 < TS:
                        exps(t + 2)

        @block.vector
        def _(dve):
            steps = [0]

            def step(instruction):
                steps[0] += 1
                instruction.then_inc(dve_step, 1)
                dve.wait_ge(dve_step, steps[0])

            for l in range(LAYERS):
                dve.sem_inc(blended[l], G_CREDIT)
                for free in (turned[l], turned_cp[l], conv_mm[l]):
                    dve.sem_inc(free, CREDIT)
                dve.sem_inc(acc_cp[l], 1)
            for free in (expd, o_pe, y_pe, out_free):
                dve.sem_inc(free, CREDIT)
            dve.sem_inc(p_pe, P_CREDIT)
            dve.sem_inc(p_dve, 1)
            dve.sem_inc(p_act, 1)
            dve.sem_inc(y_ready, Y_CREDIT)
            dve.sem_inc(out_ready, OUT_CREDIT)
            dve.memset(zeros[:], 0.0).then_inc(consts_dve, 1)
            dve.memset(ones[:], 1.0).then_inc(consts_dve, 1)
            dve.memset(qk_T[:], 0.0).then_inc(consts_dve, 1)

            dve.wait_ge(consts, CONSTS)
            step(dve.tensor_scalar(grid_i[:, 0:1], grid_i[:, 0:1], W - 1, None, ALU.bitwise_and))
            step(dve.tensor_scalar(grid_i[:, 1:2], grid_i[:, 1:2], W.bit_length() - 1, None,
                                   ALU.logical_shift_right))
            dve.tensor_copy(gridw[:], grid_i[:, 0:1])
            dve.tensor_scalar(gridn[:], grid_i[:, 1:2], float(HW), float(W + 1), ALU.mult, ALU.add)
            step(dve.tensor_copy(gridh[:], grid_i[:, 2:2 + H]))

            def sample_rows_and_weights(l):
                dve.wait_ge(off_pe, l + 1)
                dve.wait_ge(setup_cp, 1)
                bias = rowb[:, BIAS[l]:BIAS[l] + NOFF]
                step(dve.tensor_tensor(OFF[:], off_acc.rearrange("p (h j) -> p h j", j=NOFF),
                                       bias.unsqueeze(1).broadcast_to([P, H, NOFF]), ALU.add))
                dve.tensor_tensor(base[:, 0, :], OFF[:, :, 4], gridh[:], ALU.add)
                step(dve.tensor_scalar(base[:, 1, :], OFF[:, :, 5], gridw[:], None, ALU.add))
                for a in range(2):
                    dve.tensor_tensor(rowpos[:, a, 0, :], base[:, a, :], OFF[:, :, 2 * a], ALU.subtract)
                    dve.tensor_copy(rowpos[:, a, 1, :], base[:, a, :])
                    last = dve.tensor_tensor(rowpos[:, a, 2, :], base[:, a, :], OFF[:, :, 2 * a], ALU.add)
                step(last)
                for a in range(2):
                    for dy in range(KH):
                        src = rowpos[:, a, dy, :].rearrange("p (g i) -> p g i", i=ROWS)
                        cross = OFF[:, :, 2 * a + 1].rearrange("p (g i) -> p g i", i=ROWS)
                        dst = pos[:, a, :].rearrange("p (g k i) -> p k g i", k=TAPS, i=ROWS)
                        dve.tensor_tensor(dst[:, KH * dy], src, cross, ALU.subtract)
                        dve.tensor_copy(dst[:, KH * dy + 1], src)
                        last = dve.tensor_tensor(dst[:, KH * dy + 2], src, cross, ALU.add)
                step(last)
                step(dve.tensor_scalar(low[:], pos[:], -0.5, 0.0, ALU.add, ALU.max))
                step(dve.tensor_scalar(low[:], low[:], float(H - 2), ROUND, ALU.min, ALU.add))
                step(dve.tensor_scalar(low[:], low[:], -ROUND, None, ALU.add))
                step(dve.scalar_tensor_tensor(rowf[:], low[:, 0, :], float(W), low[:, 1, :], ALU.mult, ALU.add))
                dve.tensor_scalar(rowi[:], rowf[:], gridn[:], None, ALU.add).then_inc(rows_ready, 1)
                step(dve.tensor_tensor(dist[:], pos[:], low[:], ALU.subtract))
                for e in range(2):
                    step(dve.tensor_scalar(hat_t[:], dist[:], -1.0, 1.0 + e, ALU.mult, ALU.add))
                    step(dve.scalar_tensor_tensor(hat[:, e], dist[:], 1.0 - e, hat_t[:], ALU.add, ALU.min))
                    step(dve.tensor_scalar(hat[:, e], hat[:, e], 0.0, None, ALU.max))
                for s, (dy, dx) in enumerate(CORNERS):
                    last = dve.tensor_tensor(wgt[:, :, s], hat[:, dy, 0, :], hat[:, dx, 1, :], ALU.mult)
                last.then_inc(wgt_ready, 1)

            for l in range(LAYERS):
                for n in range(N):
                    dve.wait_ge(xt_pe, l * 2 * N + 2 * n + 1)
                    if l and n == 0:
                        dve.wait_ge(table_out[0], 16 * 4 * N)
                    dve.tensor_copy(XT[:, n * TS:n * TS + 4, :], bank[0][:]).then_inc(xt_dve, 1)
                sample_rows_and_weights(l)
                dve.wait_ge(wgt_ready, l + 1)

                def group_stats(it, b):
                    dve.wait_ge(acc_cp[l], it * BODY + (b + 1 + 1))
                    dve.bn_stats(stats[:, ds(it * BODY + b, 1), :].rearrange("p g s -> p (g s)"),
                                 A[l][:, ds(it * (BODY * GCOL) + b * GCOL, GCOL)]).then_inc(acc_stats[l], 1)

                with dve.Fori(0, GROUPS // BODY) as it:
                    for kb in range(BODY * TAPS):
                        dve.wait_ge(gathered[l][kb % UNITS], it * (16 * ROWS * BODY * TAPS // UNITS)
                                    + 16 * ROWS * (kb // UNITS + 1))
                        dve.wait_ge(scaled[l], it * (BODY * TAPS) + (kb + 1))
                        for s in range(1, 4):
                            if s > 1:
                                dve.wait_ge(corner[l], it * (2 * BODY * TAPS) + (2 * kb + s - 1))
                            for r in range(ROWS):
                                last = dve.scalar_tensor_tensor(
                                    V[:, kb % 2, r, :], G[:, kb % UNITS, r, s * C:(s + 1) * C],
                                    wgt[:, ds(it * (BODY * GT) + (kb * ROWS + r), 1), s],
                                    V[:, kb % 2, r, :], ALU.mult, ALU.add)
                            last.then_inc(corner[l] if s < 3 else blended[l], 1)
                        if kb == TAPS + 1:
                            group_stats(it, 0)
                    group_stats(it, 1)

                dve.wait_ge(acc_stats[l], GROUPS)
                step(dve.bn_aggr(mv[:], stats[:].rearrange("p g s -> p (g s)")))
                dve.tensor_scalar(veps, mv[:, 1:2], BN_EPS, None, ALU.add).then_inc(var_ready, 1)
                dve.wait_ge(root_ready, l + 1)
                dve.wait_ge(var_ready, l + 1)
                step(dve.reciprocal(rinv, root))
                step(dve.tensor_tensor(sq, rinv, rinv, ALU.mult))
                step(dve.tensor_tensor(corr, sq, veps, ALU.mult))
                step(dve.tensor_scalar(corr, corr, -0.5, 1.5, ALU.mult, ALU.add))
                step(dve.tensor_tensor(rinv, rinv, corr, ALU.mult))
                step(dve.tensor_tensor(bn_scale, rinv, bn[l][:, 0:1], ALU.mult))
                step(dve.tensor_tensor(mscale, mv[:, 0:1], bn_scale, ALU.mult))
                dve.tensor_tensor(bn_shift, bn[l][:, 1:2], mscale, ALU.subtract).then_inc(norm_ready, 1)
                if l == 0:
                    dve.wait_ge(norm_ready, 1)
                    dve.wait_ge(acc_cp[0], GROUPS + 1)
                    step(dve.tensor_scalar(XH[:], A[0][:], bn_scale, bn_shift, ALU.mult, ALU.add))
                    dve.tensor_scalar(XH[:], XH[:], 0.0, None, ALU.max).then_inc(xh_ready, 1)

            dve.wait_ge(norm_ready, LAYERS)
            dve.wait_ge(acc_cp[1], GROUPS + 1)
            with dve.Fori(0, N) as n:
                dve.wait_ge(out_ready, n * 2 + OUT_CREDIT)
                dve.scalar_tensor_tensor(
                    F[:].rearrange("c (h w) -> c h w", w=W),
                    A[1][:].rearrange("c (h q) -> c h q", h=H)[:, :, ds(n * W, W)], bn_scale,
                    X[:, ds(n * HW, HW)].rearrange("c (h w) -> c h w", w=W), ALU.mult, ALU.add).then_inc(res_add, 1)
                dve.wait_ge(v_pe, n + 1)
                dve.tensor_tensor(vT[:], pair[1][:].rearrange("p (t c) -> p t c", c=C),
                                  rowb[:, BV:BV + C].unsqueeze(1).broadcast_to([P, TS, C]), ALU.add).then_inc(v_cp, 1)

                def maxes(t):
                    dve.wait_ge(score, n * TS + (t + 1))
                    dve.wait_ge(expd, n * TS + (t + 1))
                    dve.tensor_reduce(nmax[:, t % 2:t % 2 + 1], pair[t % 2][:], axis=AX.X, op=ALU.max,
                                      negate=True).then_inc(maxed, 1)

                def normalise(t):
                    dve.wait_ge(expd, n * TS + (t + 1 + CREDIT))
                    dve.reciprocal(einv[:, t % 2:t % 2 + 1], esum[:, t % 4:t % 4 + 1]).then_inc(einv_ready, 1)
                    dve.wait_ge(o_pe, n * TS + (t + 1 + CREDIT))
                    dve.wait_ge(y_pe, n * TS + (t + 1))
                    dve.wait_ge(einv_ready, n * TS + (t + 1))
                    dve.tensor_scalar(yT[:, t % 2, :], bank[2][:, 0:P],
                                      einv[:, t % 2:t % 2 + 1], rowb[:, GAM:GAM + 1], ALU.mult,
                                      ALU.mult).then_inc(y_ready, 1)

                def finish(half):
                    dve.wait_ge(y_pe, n * TS + (4 * half + 4 + CREDIT))
                    dve.wait_ge(out_free, n * 2 + (half + 1))
                    dve.tensor_tensor(OUT[:, half, :], bank[3][:], F[:, half * BANK:(half + 1) * BANK],
                                      ALU.add).then_inc(out_ready, 1)

                maxes(0)
                maxes(1)
                for t in range(TS):
                    dve.wait_ge(p_pe, n * (2 * TS) + (2 * t + 1 + P_CREDIT))
                    dve.wait_ge(o_pe, n * TS + (t + 1))
                    dve.tensor_copy(prob[:, t % 2, 0:4, :], bank[0][:]).then_inc(p_dve, 1)
                    if t + 2 < TS:
                        maxes(t + 2)
                    if t == 6:
                        finish(0)
                    if t:
                        normalise(t - 1)
                normalise(TS - 1)
                finish(1)

        @block.tensor
        def _(pe):
            def transposes(bank_cols, tiles):
                for j, tile in enumerate(tiles):
                    last = pe.transpose(bank_cols[:, j * P:(j + 1) * P], tile, ident)
                return last

            pe.wait_ge(consts, CONSTS)
            for l in range(LAYERS):
                if l:
                    pe.wait_ge(turned_cp[0], CREDIT + GROUPS * TAPS)
                for n in range(N):
                    if l == 0:
                        pe.wait_ge(x_in[n], 16)
                    else:
                        pe.wait_ge(bn_done, n + 1)
                    for half, copied in enumerate((xt_dve, xt_act)):
                        if l or n:
                            pe.wait_ge(copied, l * N + n)
                        transposes(bank[half], [tile_cols(l, n, 4 * half + j) for j in range(4)]) \
                            .then_inc(xt_pe, 1)
                if l == 0:
                    pe.wait_ge(offw_in, 16 * 2 * LAYERS)
                    pe.wait_ge(small_in, 16 * SMALL)
                    pe.wait_ge(consts_dve, 3)
                    for m in range(LAYERS):
                        w = off_nat[m][:].rearrange("o (c k) -> o k c", k=TAPS)
                        for k in range(TAPS):
                            at = (m * TAPS + k) * NOFF
                            pe.transpose(pair[1][:, at:at + NOFF], w[:, k, :], ident[0:NOFF, 0:NOFF])
                    pe.matmul(pair[1][:, 128:128 + ROWLEN], ones[:], row[:], start=True, stop=True)
                    pe.transpose(pair[1][:, 320:320 + D], qkv_nat[0:D, 0, :], ident[0:D, 0:D])
                    pe.transpose(pair[1][:, 352:352 + D], qkv_nat[0:D, 1, :], ident[0:D, 0:D])
                    pe.transpose(pair[1][:, 384:512], qkv_nat[:, 2, :], ident).then_inc(setup_pe, 1)
                    pe.wait_ge(setup_cp, 1)
                pe.wait_ge(xh_ready, N + l)
                for q in range(4):
                    if q > 1 or l:
                        pe.wait_ge(z_act, l * 4 + q - 1)
                    for j in range(8):
                        last = pe.matmul(bank[2 + q % 2][:, j * TAPS * NOFF:(j + 1) * TAPS * NOFF],
                                         XH[:, (q * 8 + j) * P:(q * 8 + j + 1) * P], off_T[l][:], start=True, stop=True)
                    last.then_inc(z_pe, 1)
                pe.wait_ge(z_act, (l + 1) * 4)
                order = [(0, 0)] + [(dy, dx) for dy in (-1, 0, 1) for dx in (-1, 0, 1) if (dy, dx) != (0, 0)]
                for j, (dy, dx) in enumerate(order):
                    h0, h1 = max(0, -dy), H - max(0, dy)
                    k = (dy + 1) * KH + dx + 1
                    last = pe.matmul(off_acc.rearrange("p (h j) -> p h j", j=NOFF)[:, h0:h1, :], shift[:, dx + 1, :],
                                     ZS[:, h0 + dy:h1 + dy, k * NOFF:(k + 1) * NOFF],
                                     start=(j == 0), stop=(j == TAPS - 1))
                last.then_inc(off_pe, 1)
                if l == 0:
                    pe.wait_ge(dcnw_in, 16 * LAYERS)
                    for m in range(LAYERS):
                        w = dcn_nat[m][:].rearrange("o (c k) -> o k c", k=TAPS)
                        if m:
                            pe.wait_ge(setup_cp, 1 + m)
                        transposes(bank[2], [w[:, k, :] for k in range(0, 4)])
                        transposes(bank[3], [w[:, k, :] for k in range(4, 8)])
                        transposes(pair[1], [w[:, 8, :]]).then_inc(setup_pe, 1)
                    pe.wait_ge(setup_cp, 1 + LAYERS)

                def turn(it, kb):
                    pe.wait_ge(blended[l], it * (BODY * TAPS) + (kb + 1 + G_CREDIT))
                    pe.wait_ge(turned_cp[l], it * (BODY * TAPS) + (kb + 1))
                    transposes(bank[kb % 2], [V[:, kb % 2, r, :] for r in range(ROWS)]).then_inc(turned[l], 1)

                def convolve(it, kb):
                    k = kb % TAPS
                    if k == 0:
                        pe.wait_ge(acc_cp[l], it * BODY + (kb // TAPS + 1))
                    pe.wait_ge(turned_cp[l], it * (BODY * TAPS) + (kb + 1 + CREDIT))
                    pe.matmul(conv_acc, dcn_T[l][:, k, :], CT[:, kb % 2, :], start=(k == 0),
                              stop=(k == TAPS - 1)).then_inc(conv_mm[l], 1)

                with pe.Fori(0, GROUPS // BODY) as it:
                    for kb in range(BODY * TAPS):
                        turn(it, kb)
                        if kb:
                            convolve(it, kb - 1)
                    convolve(it, BODY * TAPS - 1)

            pe.wait_ge(turned_cp[1], CREDIT + GROUPS * TAPS)
            pe.wait_ge(acc_cp[1], GROUPS + 1)
            with pe.Fori(0, N) as n:
                pe.wait_ge(f_ready, n + 1)
                pe.wait_ge(expd, n * TS + CREDIT)
                for half in range(2):
                    last = pe.matmul(pair[0][0:48, half * BANK:(half + 1) * BANK], qk_T[:, 0:48],
                                     F[:, half * BANK:(half + 1) * BANK], start=True, stop=True)
                last.then_inc(qk_pe, 1)
                for t in range(TS):
                    last = pe.matmul(pair[1][:, t * P:(t + 1) * P], F[:, t * P:(t + 1) * P], wv_T[:],
                                     start=True, stop=True)
                last.then_inc(v_pe, 1)

                def scores(t):
                    for half in range(2):
                        last = pe.matmul(pair[t % 2][:, half * BANK:(half + 1) * BANK],
                                         qk[:, 1, t * P:(t + 1) * P],
                                         qk[:, 0, half * BANK:(half + 1) * BANK], start=True, stop=True)
                    last.then_inc(score, 1)

                def attend(t):
                    pe.wait_ge(p_dve, n * TS + (t + 1 + 1))
                    pe.wait_ge(p_act, n * TS + (t + 1 + 1))
                    pe.wait_ge(y_ready, n * TS + (t + Y_CREDIT))
                    for j in range(TS):
                        last = pe.matmul(bank[2][:, 0:P], prob[:, t % 2, j, :],
                                         vT[:, j, :], start=(j == 0), stop=(j == TS - 1))
                    last.then_inc(o_pe, 1)

                def output_turn(t):
                    pe.wait_ge(y_ready, n * TS + (t + 1 + Y_CREDIT))
                    if t % 4 == 0:
                        pe.wait_ge(out_ready, n * 2 + (t // 4 + OUT_CREDIT))
                    pe.transpose(bank[3][:, (t % 4) * P:(t % 4 + 1) * P], yT[:, t % 2, :], ident).then_inc(y_pe, 1)

                pe.wait_ge(qk_cp, n * 2 + 2)
                scores(0)
                pe.wait_ge(v_cp, n + 1)
                scores(1)
                for t in range(TS):
                    pe.wait_ge(expd, n * TS + (t + 1 + CREDIT))
                    for half, copied in enumerate((p_dve, p_act)):
                        pe.wait_ge(copied, n * TS + (t + 1))
                        transposes(bank[half], [probT[:, t % 2, (4 * half + j) * P:(4 * half + j + 1) * P]
                                                for j in range(4)]).then_inc(p_pe, 1)
                    if t + 2 < TS:
                        scores(t + 2)
                    if t:
                        attend(t - 1)
                    if t > 1:
                        output_turn(t - 2)
                attend(TS - 1)
                output_turn(TS - 2)
                output_turn(TS - 1)


_LAYER = ['tm{}_w', 'tm{}_b', 'tr{}_w', 'tr{}_b', 'dcn{}_w', 'bn{}_g', 'bn{}_b']
_ATTN = ['wq', 'bq', 'wk', 'bk', 'wv', 'bv', 'gamma']


def kernel(**inputs):
    import numpy as _np
    import concourse.bacc as _bacc
    from concourse import mybir as _mybir
    from concourse.bass_utils import run_bass_kernel_spmd as _run

    nc = _bacc.Bacc("TRN2", target_bir_lowering=False, num_devices=1)
    arrays = {}

    def dram(name):
        a = _np.ascontiguousarray(inputs[name])
        if a.ndim == 0:
            a = a.reshape(1)
        arrays[f"in_{name}_dram"] = a
        return nc.dram_tensor(f"in_{name}_dram", a.shape, _mybir.dt.from_np(a.dtype), kind="ExternalInput").ap()

    x = dram("x")
    layers = [[dram("L0_conv_" + name.format(l)) for l in (1, 2)] for name in _LAYER]
    attn = [dram("L1_conv_" + name) for name in _ATTN]
    n, c, h, w = inputs["x"].shape
    out = nc.dram_tensor("out_0_dram", (n, c, h, w), _mybir.dt.float32, kind="ExternalOutput").ap()
    table = nc.dram_tensor("table", [n * h * w + w + 1, 4 * c], _mybir.dt.float32)
    deform_resblock_attention(nc, x, *layers, *attn, out, table)
    r = _run(nc, [arrays], core_ids=[0])
    return r.results[0]["out_0_dram"]
```

```python
import concourse.bass as bass
from concourse import mybir
from contextlib import ExitStack


def deform_resblock_attention(nc, x, tm_w, tm_b, tr_w, tr_b, dcn_w, bn_g, bn_b,
                              wq, bq, wk, bk, wv, bv, gamma, out, tables):
    f32, i32, bf16 = mybir.dt.float32, mybir.dt.int32, mybir.dt.bfloat16
    ALU, ACT, AX = mybir.AluOpType, mybir.ActivationFunctionType, mybir.AxisListType
    ds = bass.ds

    N, C, H, W = x.shape
    HW = H * W
    PIX = N * HW
    P = 128
    assert N * W == P and C == P
    KH = 3
    TAPS = KH * KH
    NOFF = 6
    BANK = 512
    TS = HW // P
    TROWS = P // W
    GTILES = BANK // P
    IGROUPS = TS // GTILES
    GROUPS = N * IGROUPS
    GT = TAPS * GTILES
    ITILES = IGROUPS * GT
    TILES = GROUPS * GT
    IBLOCKS = IGROUPS * TAPS
    CORNERS = [(0, 0), (0, 1), (1, 0), (1, 1)]
    UNITS = 6
    ROUND = 12582912.0
    REACH = P - W
    BN_EPS = 1e-5
    D = wq.shape[0]
    LAYERS = 2
    BV = LAYERS * NOFF
    GAM = BV + C
    ROWLEN = GAM + 1
    Q_PARTS = "hhmmhl"
    K_PARTS = "hmhmlh"
    STACK = len(Q_PARTS) * D
    KROWS = STACK + 3

    with ExitStack() as ctx:
        def sb(name, shape, dt=f32):
            return ctx.enter_context(nc.sbuf_tensor(name, shape, dt))

        def sem(name):
            return ctx.enter_context(nc.semaphore(name))

        X = sb("X", [P, PIX])
        A = [sb(f"A{l}", [P, PIX]) for l in range(LAYERS)]
        XN = [X, A[1]]
        XT = sb("XT", [P, PIX // P, C])
        ZS = sb("ZS", [P, KH, TS, KH * NOFF])
        US = sb("US", [P, TS, KH, NOFF])
        OFT = sb("OFT", [P, N, TS, NOFF])
        band = sb("band", [P, KH, 2 * REACH + P])
        ident = band[:, 1, REACH:REACH + P]
        identb = sb("identb", [P, P], bf16)
        zeros = sb("zeros", [P, 4 * C])
        ones = sb("ones", [1, P])
        grid_i = sb("grid_i", [P, 2], i32)
        gridw = sb("gridw", [P, 1])
        gridr = sb("gridr", [P, 1])
        tile_i = sb("tile_i", [P, TS], i32)
        gridh = sb("gridh", [P, TS])
        base = sb("base", [P, 2, N * TS])
        rowpos = sb("rowpos", [P, 2, KH, N * TS])
        pos = sb("pos", [P, 2, TILES])
        low = sb("low", [P, 2, TILES])
        dist = sb("dist", [P, 2, TILES])
        hat = sb("hat", [P, 2, 2, TILES])
        upper = sb("upper", [P, 2, TILES])
        wgt = sb("wgt", [P, TILES, 4])
        rowf = sb("rowf", [P, TILES])
        rowi = sb("rowi", [P, TILES], i32)
        rows_now = sb("rows_now", [P, IGROUPS, GT], i32)
        G = sb("G", [P, UNITS, GTILES, 4 * C])
        V = sb("V", [P, 2, GTILES, C])
        CT = sb("CT", [P, 2, BANK])
        dcn_nat = [sb(f"dcn_nat{l}", [P, C * TAPS]) for l in range(LAYERS)]
        dcn_T = [sb(f"dcn_T{l}", [P, TAPS, P]) for l in range(LAYERS)]
        off_nat = [sb(f"off_nat{l}", [NOFF, C * TAPS]) for l in range(LAYERS)]
        off_T = [sb(f"off_T{l}", [P, TAPS * NOFF]) for l in range(LAYERS)]
        row = sb("row", [1, ROWLEN])
        rowb = sb("rowb", [P, ROWLEN])
        bn = [sb(f"bn{l}", [P, 2]) for l in range(LAYERS)]
        stats = sb("stats", [P, GROUPS, 6])
        mv = sb("mv", [P, 2])
        nrm = sb("nrm", [P, 8])
        veps = nrm[:, 0:1]
        root = nrm[:, 1:2]
        rinv = nrm[:, 2:3]
        sq = nrm[:, 3:4]
        corr = nrm[:, 4:5]
        bn_scale = nrm[:, 5:6]
        mscale = nrm[:, 6:7]
        bn_shift = nrm[:, 7:8]
        warm = sb("warm", [1, 1])
        qkv_nat = sb("qkv_nat", [P, 3, C])
        qk_T = sb("qk_T", [P, 2, STACK])
        wv_T = sb("wv_T", [P, C])
        cols_row = sb("cols_row", [1, 6, STACK])
        cols = sb("cols", [STACK, 6])
        nmax = sb("nmax", [P, N, TS])
        nmax_r = sb("nmax_r", [P, 2, TS])
        nmax_p = sb("nmax_p", [P, 2, 3, TS], bf16)
        einv = sb("einv", [P, N, TS])
        stacks = sb("stacks", [P, N, 2, HW], bf16)
        yT = sb("yT", [P, TS, C])
        F = A[1]
        probs = A[0][:].rearrange("p (r k) -> p r k", r=4)
        PRING = 4
        qk32 = XT[0:STACK, 0:2 * TS, :].rearrange("p (b t) k -> p b (t k)", b=2)
        resid = XT[0:STACK, 2 * TS:4 * TS, :].rearrange("p (b t) k -> p b (t k)", b=2)
        gflat = G[:].rearrange("p a b c -> p (a b c)")
        vT = gflat[:, 0:N * TS * (C + 1)].rearrange("p (n t c) -> p n t c", n=N, t=TS)
        parts = gflat[0:STACK, 5 * HW:6 * HW].bitcast(bf16).rearrange("p (b k) -> p b k", b=2)
        OUT = gflat[:, 6 * HW:7 * HW].rearrange("p (b k) -> p b k", b=2)

        bank = [ctx.enter_context(nc.psum_tensor(f"bank{i}", [P, BANK], f32)) for i in range(4)]
        pair = [ctx.enter_context(nc.psum_tensor(f"pair{i}", [P, 2 * BANK], f32)) for i in range(2)]
        out_acc = bank[0:3]
        misc = bank[3]
        xt_acc = bank[2:4]
        conv_acc = pair[0][:, 0:BANK]
        setup_acc = pair[0][:, BANK:2 * BANK]
        z_acc = pair[1][:, 0:TS * TAPS * NOFF]
        u_acc = pair[1][:, BANK:BANK + TS * KH * NOFF]
        off_acc = pair[1][:, BANK + TS * KH * NOFF:BANK + TS * (KH + 1) * NOFF]

        x_in = [sem(f"x_in{n}") for n in range(N)]
        offw_in = [sem(f"offw_in{l}") for l in range(LAYERS)]
        bias_in = sem("bias_in")
        dcnw_in = [sem(f"dcnw_in{m}") for m in range(LAYERS)]
        small_in = sem("small_in")
        consts = sem("consts")
        consts_dve = sem("consts_dve")
        identb_ready = sem("identb_ready")
        fill_out = sem("fill_out")
        setup_pe = sem("setup_pe")
        setup_cp = sem("setup_cp")
        xt_pe = sem("xt_pe")
        xt_dve = sem("xt_dve")
        xt_act = sem("xt_act")
        z_pe = sem("z_pe")
        z_act = sem("z_act")
        u_pe = sem("u_pe")
        u_act = sem("u_act")
        off_pe = sem("off_pe")
        off_ready = sem("off_ready")
        dve_step = sem("dve_step")
        rows_ready = sem("rows_ready")
        wgt_ready = sem("wgt_ready")
        table_out = [[sem(f"table_out{l}_{n}") for n in range(N)] for l in range(LAYERS)]
        rows_copied = sem("rows_copied")
        gathered = [[sem(f"gathered{l}_{u}") for u in range(UNITS)] for l in range(LAYERS)]
        scaled = [sem(f"scaled{l}") for l in range(LAYERS)]
        corner = [sem(f"corner{l}") for l in range(LAYERS)]
        blended = [sem(f"blended{l}") for l in range(LAYERS)]
        turned = [sem(f"turned{l}") for l in range(LAYERS)]
        turned_cp = [sem(f"turned_cp{l}") for l in range(LAYERS)]
        conv_mm = [sem(f"conv_mm{l}") for l in range(LAYERS)]
        acc_cp = [sem(f"acc_cp{l}") for l in range(LAYERS)]
        acc_stats = [sem(f"acc_stats{l}") for l in range(LAYERS)]
        var_ready = sem("var_ready")
        root_ready = sem("root_ready")
        norm_ready = sem("norm_ready")
        xn_ready = sem("xn_ready")
        res_add = sem("res_add")
        f_ready = sem("f_ready")
        ones_ready = sem("ones_ready")
        misc_full = sem("misc_full")
        misc_free = sem("misc_free")
        first_v = sem("first_v")
        qk_cp = sem("qk_cp")
        part_cast = sem("part_cast")
        resid_ready = sem("resid_ready")
        stack_ready = sem("stack_ready")
        keymax_full = sem("keymax_full")
        keymax_free = sem("keymax_free")
        score_full = sem("score_full")
        max_split = sem("max_split")
        stack_full = sem("stack_full")
        expd = sem("expd")
        weighed = sem("weighed")
        einv_ready = sem("einv_ready")
        y_ready = sem("y_ready")
        out_ready = sem("out_ready")
        out_dma = [sem(f"out_dma{i}") for i in range(2)]

        G_CREDIT = UNITS
        CREDIT = 2
        CONSTS = 1 + KH + 4
        SMALL = 2 * LAYERS + 9
        TABLE_AT = [0] + [(n - 1) * HW for n in range(1, N)]
        FILLS = 2 * 2
        MASKS = sum(p != "h" for p in Q_PARTS + K_PARTS) + (Q_PARTS + K_PARTS).count("l")

        def tile_cols(l, n, t):
            return XN[l][:, n * HW + t * P:n * HW + (t + 1) * P]

        START = {n: 3 * (n - 1) for n in range(1, N)}
        Z_FIRST = {START[n]: n for n in START}
        Z_SECOND = {START[n] + 1: n for n in START}
        TURN_SUM = {START[n] + 2: n for n in START}
        OFF_SUM = {START[n] + 3: n for n in START}
        RELU = {START[n] - 2: n for n in START}
        POSITIONS, ROWS, WEIGHTS = (START[N - 1] + 3 + i for i in (1, 2, 3))
        LATE_SETUP = {POSITIONS + i: 4 + i for i in range(4)}
        SETUPS = 8
        assert max(LATE_SETUP) < IBLOCKS and START[N - 1] + 3 < IBLOCKS

        SLOTS = range(-1, N)
        SLOT_MAX = {0: (0, 1), 1: (2, 3), 2: (4,), 3: (5,), 4: (6,), 5: (7,)}
        FIRST_MAX = {0: (0, 1, 2, 3), 1: (4, 5), 2: (6, 7)}
        SLOT_MISC = {0: (("q", 0), ("q", 1)), 1: (("k", 0),), 2: (("k", 1),), 3: (("y", 0),),
                     4: (("y", 1),), 5: (("v", 0),), 6: (("v", 1),)}

        def slot_max(s, step):
            return (FIRST_MAX if s < 0 else SLOT_MAX).get(step, ())

        def split_step(s):
            return max(FIRST_MAX if s < 0 else SLOT_MAX)

        def misc_jobs(s, step):
            for what, half in SLOT_MISC.get(step, ()):
                n = s - 1 if what == "y" else s + 2
                if 0 <= n < N:
                    yield what, n, half

        FIRST_JOBS = [(what, 0, half) for what in "qkv" for half in range(2)]
        LAST_JOBS = [("y", N - 1, half) for half in range(2)]
        JOBS = FIRST_JOBS + [j for s in SLOTS for step in range(TS) for j in misc_jobs(s, step)] + LAST_JOBS
        JOB = {job: i for i, job in enumerate(JOBS)}
        FIRST_BANK = {}
        for half in range(2):
            FIRST_BANK["q", 0, half] = pair[1][:, half * BANK:(half + 1) * BANK]
            FIRST_BANK["k", 0, half] = pair[0][:, half * BANK:(half + 1) * BANK]
            FIRST_BANK["v", 0, half] = out_acc[half][:]

        def job_bank(job):
            return FIRST_BANK[job] if job in FIRST_BANK else misc[:]

        def misc_uses(job):
            return JOB[job] - len(FIRST_JOBS)

        def keymax_pair(n, t):
            return pair[t % 2 if n == 0 else 0]

        block = ctx.enter_context(nc.Block())

        @block.sync
        def _(sp):
            for n in range(N):
                sp.dma_start(X[:, n * HW:(n + 1) * HW],
                             x[n].rearrange("c h w -> c (h w)")).then_inc(x_in[n], 16)
                if n < LAYERS:
                    sp.dma_start(dcn_nat[n][:], dcn_w[n].rearrange("o c i j -> o (c i j)")) \
                        .then_inc(dcnw_in[n], 16)
                if n == 0:
                    sp.wait_ge(consts_dve, 1)
                    for table in tables:
                        sp.dma_start(table[0:W + 1, :], zeros[0:W + 1, :]).then_inc(fill_out, 16)
                        end = table.shape[0]
                        sp.dma_start(table[end - W - 1:end, :], zeros[0:W + 1, :]).then_inc(fill_out, 16)
            sp.dma_start(off_nat[1][0:4, :], tm_w[1].rearrange("o c i j -> o (c i j)")).then_inc(offw_in[1], 16)
            sp.dma_start(off_nat[1][4:6, :], tr_w[1].rearrange("o c i j -> o (c i j)")).then_inc(offw_in[1], 16)
            sp.dma_start(row[:, NOFF:NOFF + 4], tm_b[1].rearrange("(a n) -> a n", a=1)).then_inc(small_in, 16)
            sp.dma_start(row[:, NOFF + 4:NOFF + 6], tr_b[1].rearrange("(a n) -> a n", a=1)).then_inc(small_in, 16)
            for m in range(LAYERS):
                sp.dma_start(bn[m][:, 0:1], bn_g[m].rearrange("(n a) -> n a", a=1)).then_inc(small_in, 16)
                sp.dma_start(bn[m][:, 1:2], bn_b[m].rearrange("(n a) -> n a", a=1)).then_inc(small_in, 16)
            sp.dma_start(row[:, BV:BV + C], bv.rearrange("(a n) -> a n", a=1)).then_inc(small_in, 16)
            sp.dma_start(row[:, GAM:GAM + 1], gamma.rearrange("(a n) -> a n", a=1)).then_inc(small_in, 16)
            for j, b in enumerate((bq, bk)):
                sp.dma_start(cols_row[:, j, :].rearrange("a (b d) -> a b d", d=D),
                             b.rearrange("(a u d) -> a u d", a=1, u=1)
                             .broadcast_to([1, len(Q_PARTS), D])).then_inc(small_in, 16)
            for j, w in enumerate((wq, wk, wv)):
                sp.dma_start(qkv_nat[0:w.shape[0], j, :], w).then_inc(small_in, 16)
            sp.wait_ge(fill_out, 16 * FILLS)
            for l in range(LAYERS):
                if l:
                    sp.wait_ge(blended[l - 1], G_CREDIT + GROUPS * TAPS)
                for n in range(N):
                    sp.wait_ge(xt_dve, l * N + n + 1)
                    sp.wait_ge(xt_act, l * N + n + 1)
                    for s, (dy, dx) in enumerate(CORNERS):
                        first = TABLE_AT[n] + W + 1 - (dy * W + dx)
                        sp.dma_start(tables[min(n, 1)][first:first + HW, s * C:(s + 1) * C].rearrange("(t p) c -> p t c", p=P),
                                     XT[:, n * TS:(n + 1) * TS, :]).then_inc(table_out[l][n], 16)
            for n in range(N):
                for half in range(2):
                    sp.wait_ge(out_ready, n * 2 + half + 1)
                    sp.dma_start(out[n].rearrange("c h w -> c (h w)")[:, half * BANK:(half + 1) * BANK],
                                 OUT[:, half, :]).then_inc(out_dma[half], 16)
            for half in range(2):
                sp.wait_ge(out_dma[half], 16 * N)

        @block.gpsimd
        def _(pool):
            pool.memset(band[:], 0.0).then_inc(consts, 1)
            pool.wait_ge(consts, 1)
            for j in range(KH):
                pool.affine_select(out=band[:, j, :], in_=band[:, j, :], compare_op=ALU.not_equal, fill=1.0,
                                   base=REACH - (j - 1), pattern=[[-1, 2 * REACH + P]],
                                   channel_multiplier=1).then_inc(consts, 1)
            pool.wait_ge(consts, 1 + KH)
            pool.memset(band[:, 0, :].rearrange("p (n w) -> p n w", w=W)[:, :, 0:1], 0.0).then_inc(consts, 1)
            pool.memset(band[:, 2, :].rearrange("p (n w) -> p n w", w=W)[:, :, W - 1:W], 0.0).then_inc(consts, 1)
            pool.iota(grid_i[:], pattern=[[0, 2]], base=0, channel_multiplier=1).then_inc(consts, 1)
            pool.iota(tile_i[:], pattern=[[TROWS, TS]], base=0, channel_multiplier=0).then_inc(consts, 1)
            pool.wait_ge(consts, CONSTS)
            pool.tensor_copy(identb[:], ident).then_inc(identb_ready, 1)
            pool.wait_ge(identb_ready, 1)
            def gather_image(l, it, table):
                for b in range(IGROUPS):
                    pool.wait_ge(blended[l], it * IBLOCKS + (b * TAPS + 1))
                    pool.tensor_copy(rows_now[:, b, :], rowi[:, ds(it * ITILES + b * GT, GT)]) \
                        .then_inc(rows_copied, 1)
                    pool.wait_ge(rows_copied, it * IGROUPS + (l * GROUPS + b + 1))
                    pool.nop(nofuse=True)
                    for k in range(TAPS):
                        kb = b * TAPS + k
                        if k:
                            pool.wait_ge(blended[l], it * IBLOCKS + (kb + 1))
                            pool.nop(nofuse=True)
                        for r in range(GTILES):
                            c = k * GTILES + r
                            pool.indirect_dma_start(
                                G[:, kb % UNITS, r, :], None, table[:, :],
                                bass.IndirectOffsetOnAxis(rows_now[:, b, c:c + 1], 0)) \
                                .then_inc(gathered[l][kb % UNITS], 16)

            for l in range(LAYERS):
                pool.wait_ge(rows_ready, 2 * l + 1)
                pool.wait_ge(fill_out, 16 * FILLS)
                pool.wait_ge(table_out[l][0], 16 * 4)
                gather_image(l, 0, tables[0])
                pool.wait_ge(rows_ready, 2 * l + 2)
                for n in range(1, N):
                    pool.wait_ge(table_out[l][n], 16 * 4)
                with pool.Fori(1, N) as it:
                    gather_image(l, it, tables[1])

            pool.wait_ge(turned_cp[1], CREDIT + GROUPS * TAPS)
            pool.memset(stacks[STACK:KROWS, :, 0, :], 1.0).then_inc(ones_ready, 1)
            pool.wait_ge(ones_ready, 1)
            pool.memset(vT[:, :, :, C:C + 1], 1.0).then_inc(ones_ready, 1)
            pool.wait_ge(ones_ready, 2)

        @block.scalar
        def _(act):
            act.dma_start(off_nat[0][0:4, :], tm_w[0].rearrange("o c i j -> o (c i j)")).then_inc(offw_in[0], 16)
            act.dma_start(off_nat[0][4:6, :], tr_w[0].rearrange("o c i j -> o (c i j)")).then_inc(offw_in[0], 16)
            act.dma_start(row[:, 0:4], tm_b[0].rearrange("(a n) -> a n", a=1)).then_inc(bias_in, 16)
            act.dma_start(row[:, 4:6], tr_b[0].rearrange("(a n) -> a n", a=1)).then_inc(bias_in, 16)
            act.wait_ge(consts_dve, 2)
            act.sqrt(warm[:], ones[:, 0:1])

            for l in range(LAYERS):
                def relu_input(n):
                    if l:
                        own = slice(n * HW, (n + 1) * HW)
                        act.activation(XN[1][:, own], A[0][:, own], ACT.Relu, bias=bn_shift,
                                       scale=bn_scale).then_inc(xn_ready, 1)

                def z_copy(n):
                    act.wait_ge(z_pe, l * N + n + 1)
                    act.copy(ZS[:].rearrange("p x t j -> p t x j"),
                             z_acc.rearrange("p (t x j) -> p t x j", t=TS, x=KH)).then_inc(z_act, 1)

                def u_copy(n):
                    act.wait_ge(u_pe, l * N + n + 1)
                    act.copy(US[:].rearrange("p t y j -> p (t y j)"), u_acc).then_inc(u_act, 1)

                def xt_copy(n):
                    act.wait_ge(xt_pe, 2 * (l * N + n) + 2)
                    if l:
                        act.wait_ge(table_out[0][n], 16 * 4)
                    act.copy(XT[:, n * TS + 4:(n + 1) * TS, :], xt_acc[1][:]).then_inc(xt_act, 1)

                def setup(i):
                    act.wait_ge(setup_pe, i + 1)
                    if i == 0:
                        act.copy(off_T[0][:], setup_acc[:, 0:TAPS * NOFF])
                        act.copy(rowb[:, 0:NOFF], setup_acc[:, 128:128 + NOFF])
                    elif i < 7:
                        m, third = divmod(i - 1, 3)
                        k0, k1 = (0, 4, 8, 9)[third:third + 2]
                        act.copy(dcn_T[m][:, k0:k1, :].rearrange("p k o -> p (k o)"), setup_acc[:, 0:(k1 - k0) * P])
                    else:
                        act.copy(off_T[1][:], setup_acc[:, 0:TAPS * NOFF])
                        act.copy(rowb[:, NOFF:ROWLEN], setup_acc[:, 128:128 + ROWLEN - NOFF])
                        act.copy(wv_T[:], setup_acc[:, 384:512])
                        act.copy(cols[:], setup_acc[0:STACK, 60:66])
                        for j in range(2):
                            at = 320 + j * 32
                            act.copy(qk_T[:, j, :].rearrange("p (b d) -> p b d", d=D),
                                     setup_acc[:, at:at + D].unsqueeze(1).broadcast_to([P, len(Q_PARTS), D]))
                    act.drain().then_inc(setup_cp, 1)

                if l:
                    act.wait_ge(norm_ready, 1)
                    act.wait_ge(acc_cp[0], GROUPS + 1)
                relu_input(0)
                if l == 0:
                    xt_copy(0)
                    setup(0)
                    z_copy(0)
                    u_copy(0)
                    for i in range(1, 4):
                        setup(i)
                else:
                    z_copy(0)
                    u_copy(0)
                    xt_copy(0)
                for block_no, n in RELU.items():
                    if block_no < 0:
                        relu_input(n)

                def scale(it, kb):
                    act.wait_ge(gathered[l][kb % UNITS], it * (16 * GTILES * IBLOCKS // UNITS)
                                + 16 * GTILES * (kb // UNITS + 1))
                    act.wait_ge(turned[l], it * IBLOCKS + (kb + 1))
                    for r in range(GTILES):
                        last = act.activation(
                            V[:, kb % 2, r, :], G[:, kb % UNITS, r, 0:C], ACT.Copy,
                            scale=wgt[:, ds(it * ITILES + (kb * GTILES + r), 1), 0])
                    last.then_inc(scaled[l], 1)

                def image(it, more, jobs=False):
                    for kb in range(IBLOCKS):
                        if more or kb + 1 < IBLOCKS:
                            scale(it, kb + 1)
                        act.wait_ge(turned[l], it * IBLOCKS + (kb + 1 + CREDIT))
                        act.wait_ge(conv_mm[l], it * IBLOCKS + (kb + 1))
                        act.copy(CT[:, kb % 2, :], bank[kb % 2][:]).then_inc(turned_cp[l], 1)
                        if kb % TAPS == TAPS - 1:
                            act.wait_ge(conv_mm[l], it * IBLOCKS + (kb + 1 + CREDIT))
                            act.copy(A[l][:, ds(it * HW + kb // TAPS * BANK, BANK)], conv_acc) \
                                .then_inc(acc_cp[l], 1)
                        if jobs:
                            if kb in Z_SECOND:
                                z_copy(Z_SECOND[kb])
                            if kb in TURN_SUM:
                                xt_copy(TURN_SUM[kb])
                                u_copy(TURN_SUM[kb])
                            if kb in RELU:
                                relu_input(RELU[kb])
                            if l == 0 and kb in LATE_SETUP:
                                setup(LATE_SETUP[kb])
                            if kb == IBLOCKS - 2:
                                act.wait_ge(wgt_ready, 2 * l + 2)

                act.wait_ge(wgt_ready, 2 * l + 1)
                scale(0, 0)
                image(0, True, jobs=True)
                with act.Fori(1, N - 1) as it:
                    image(it, True)
                image(N - 1, False)

                act.wait_ge(var_ready, l + 1)
                act.sqrt(root, veps).then_inc(root_ready, 1)

            act.activation(warm[:], ones[:, 0:1], ACT.Exp)
            act.wait_ge(norm_ready, 2)

            def relu(n):
                for half in range(2):
                    own = slice(n * HW + half * BANK, n * HW + (half + 1) * BANK)
                    act.wait_ge(res_add, 2 * n + half + 1)
                    act.activation(F[:, own], F[:, own], ACT.Relu, bias=bn_shift).then_inc(f_ready, 1)

            def misc_copy(job):
                what, n, half = job
                if what in "qk":
                    j = "qk".index(what)
                    if n:
                        act.wait_ge(stack_ready, 2 * (n - 1) + j + 1)
                    act.wait_ge(misc_full, JOB[job] + 1)
                    act.activation(qk32[:, j, half * BANK:(half + 1) * BANK], job_bank(job)[0:STACK], ACT.Identity,
                                   bias=cols[:, j:j + 1]).then_inc(qk_cp, 1)
                    if n:
                        act.wait_ge(qk_cp, 4 * n + 2 * j + half + 1)
                        act.sem_inc(misc_free, 1)

            def high(n, j):
                act.wait_ge(qk_cp, 4 * n + 2 * j + 2)
                act.copy(parts[:, j, :], qk32[:, j, :]).then_inc(part_cast, 1)

            def middle(n, j):
                act.wait_ge(resid_ready, 2 * n + j + 1)
                act.copy(parts[:, j, :], resid[:, j, :]).then_inc(part_cast, 1)

            def exps(n, j):
                i = n * TS + j
                act.wait_ge(score_full, i + 1)
                if i >= PRING:
                    act.wait_ge(weighed, i - PRING + 1)
                act.activation(probs[:, i % PRING, :], pair[1][:], ACT.Exp).then_inc(expd, 1)

            relu(0)
            relu(1)
            for job in FIRST_JOBS:
                misc_copy(job)
                if job[0] in "qk" and job[2] == 1:
                    high(0, "qk".index(job[0]))
            middle(0, 0)
            middle(0, 1)
            for s in SLOTS:
                for step in range(TS):
                    if s >= 0 and step + 1 < TS:
                        exps(s, step + 1)
                    for job in misc_jobs(s, step):
                        misc_copy(job)
                    if s + 2 < N and step in (1, 2):
                        high(s + 2, step - 1)
                    if s + 2 < N and step in (3, 4):
                        middle(s + 2, step - 3)
                    if s + 1 < N and step == split_step(s) + 1:
                        act.wait_ge(keymax_full, (s + 1) * (TS + 1) + TS + 1)
                        act.copy(stacks[STACK:KROWS, s + 1, 1, :], pair[0][STACK:KROWS, :]) \
                            .then_inc(stack_full, 1)
                    if s + 1 < N and step == 7:
                        exps(s + 1, 0)
                    if s + 3 < N and step == 5:
                        relu(s + 3)

        @block.vector
        def _(dve):
            steps = [0]

            def step(instruction):
                steps[0] += 1
                instruction.then_inc(dve_step, 1)
                dve.wait_ge(dve_step, steps[0])

            dve.memset(zeros[:], 0.0).then_inc(consts_dve, 1)
            dve.memset(ones[:], 1.0).then_inc(consts_dve, 1)
            for l in range(LAYERS):
                dve.sem_inc(blended[l], G_CREDIT)
                for free in (turned[l], turned_cp[l], conv_mm[l]):
                    dve.sem_inc(free, CREDIT)
                dve.sem_inc(acc_cp[l], 1)

            step(dve.memset(cols_row[:, 2:6, :], 0.0))
            for j, held in enumerate((Q_PARTS, K_PARTS)):
                for b, part in enumerate(held):
                    at = slice(b * D, (b + 1) * D)
                    if part != "h":
                        dve.memset(cols_row[:, 2 + j, at], -1.0).then_inc(consts_dve, 1)
                    if part == "l":
                        dve.memset(cols_row[:, 4 + j, at], -1.0).then_inc(consts_dve, 1)

            dve.wait_ge(consts, CONSTS)
            step(dve.tensor_scalar(grid_i[:, 0:1], grid_i[:, 0:1], W - 1, None, ALU.bitwise_and))
            step(dve.tensor_scalar(grid_i[:, 1:2], grid_i[:, 1:2], W.bit_length() - 1, None,
                                   ALU.logical_shift_right))
            dve.tensor_copy(gridw[:], grid_i[:, 0:1])
            dve.tensor_copy(gridr[:], grid_i[:, 1:2])
            step(dve.tensor_copy(gridh[:], tile_i[:]))
            step(dve.tensor_scalar(gridh[:], gridh[:], gridr[:], None, ALU.add))

            def tile_range(n0, n1):
                return slice(n0 * ITILES, n1 * ITILES)

            def positions(n0, n1):
                tiles = tile_range(n0, n1)
                off = OFT[:, n0:n1, :, :].rearrange("p n t j -> p j (n t)")
                cur = slice(n0 * TS, n1 * TS)
                dve.tensor_tensor(base[:, 0, cur].rearrange("p (n t) -> p n t", t=TS), OFT[:, n0:n1, :, 4],
                                  gridh[:].unsqueeze(1).broadcast_to([P, n1 - n0, TS]), ALU.add)
                step(dve.tensor_scalar(base[:, 1, cur], off[:, 5], gridw[:], None, ALU.add))
                dve.tensor_tensor(rowpos[:, :, 0, cur], base[:, :, cur], off[:, 0:4:2], ALU.subtract)
                dve.tensor_copy(rowpos[:, :, 1, cur], base[:, :, cur])
                step(dve.tensor_tensor(rowpos[:, :, 2, cur], base[:, :, cur], off[:, 0:4:2], ALU.add))
                for a in range(2):
                    src = rowpos[:, a, :, cur].rearrange("p e (g i) -> p e g i", i=GTILES)
                    cross = off[:, 2 * a + 1].rearrange("p (g i) -> p g i", i=GTILES).unsqueeze(1) \
                        .broadcast_to([P, KH, (n1 - n0) * IGROUPS, GTILES])
                    dst = pos[:, a, tiles].rearrange("p (g e d i) -> p d e g i", e=KH, d=KH, i=GTILES)
                    dve.tensor_tensor(dst[:, 0], src, cross, ALU.subtract)
                    dve.tensor_copy(dst[:, 1], src)
                    last = dve.tensor_tensor(dst[:, 2], src, cross, ALU.add)
                step(last)

            def sample_rows(n0, n1):
                tiles = tile_range(n0, n1)
                step(dve.tensor_scalar(low[:, :, tiles], pos[:, :, tiles], -0.5, 0.0, ALU.add, ALU.max))
                step(dve.tensor_scalar(low[:, :, tiles], low[:, :, tiles], float(H - 2), ROUND, ALU.min, ALU.add))
                step(dve.tensor_scalar(low[:, :, tiles], low[:, :, tiles], -ROUND, None, ALU.add))
                step(dve.scalar_tensor_tensor(rowf[:, tiles], low[:, 0, tiles], float(W), low[:, 1, tiles],
                                              ALU.mult, ALU.add))
                for n in range(n0, n1):
                    own = tile_range(n, n + 1)
                    last = dve.tensor_scalar(rowi[:, own], rowf[:, own], float(TABLE_AT[n] + W + 1), None, ALU.add)
                last.then_inc(rows_ready, 1)

            def bilinear_weights(n0, n1):
                tiles = tile_range(n0, n1)
                step(dve.tensor_tensor(dist[:, :, tiles], pos[:, :, tiles], low[:, :, tiles], ALU.subtract))
                for e in range(2):
                    dve.tensor_scalar(hat[:, e, :, tiles], dist[:, :, tiles], -1.0, 1.0 + e, ALU.mult, ALU.add)
                    step(dve.tensor_scalar(upper[:, :, tiles], dist[:, :, tiles], 1.0 - e, 0.0, ALU.add, ALU.max))
                    step(dve.tensor_tensor(hat[:, e, :, tiles], hat[:, e, :, tiles], upper[:, :, tiles], ALU.min))
                    step(dve.tensor_scalar(hat[:, e, :, tiles], hat[:, e, :, tiles], 0.0, None, ALU.max))
                for s, (dy, dx) in enumerate(CORNERS):
                    last = dve.tensor_tensor(wgt[:, tiles, s], hat[:, dy, 0, tiles], hat[:, dx, 1, tiles], ALU.mult)
                last.then_inc(wgt_ready, 1)

            for l in range(LAYERS):
                def xt_copy(n):
                    dve.wait_ge(xt_pe, 2 * (l * N + n) + 1)
                    if l:
                        dve.wait_ge(table_out[0][n], 16 * 4)
                    dve.tensor_copy(XT[:, n * TS:n * TS + 4, :], xt_acc[0][:]).then_inc(xt_dve, 1)

                def add_bias(n):
                    dve.wait_ge(off_pe, l * N + n + 1)
                    dve.tensor_tensor(OFT[:, n, :, :], off_acc.rearrange("p (t j) -> p t j", j=NOFF),
                                      rowb[:, l * NOFF:(l + 1) * NOFF].unsqueeze(1).broadcast_to([P, TS, NOFF]),
                                      ALU.add).then_inc(off_ready, 1)

                xt_copy(0)
                dve.wait_ge(setup_cp, SETUPS if l else 1)
                add_bias(0)
                dve.wait_ge(off_ready, l * N + 1)
                positions(0, 1)
                sample_rows(0, 1)
                bilinear_weights(0, 1)
                dve.wait_ge(wgt_ready, 2 * l + 1)

                def blend(it, kb):
                    dve.wait_ge(gathered[l][kb % UNITS], it * (16 * GTILES * IBLOCKS // UNITS)
                                + 16 * GTILES * (kb // UNITS + 1))
                    dve.wait_ge(scaled[l], it * IBLOCKS + (kb + 1))
                    for s in range(1, 4):
                        if s > 1:
                            dve.wait_ge(corner[l], it * (2 * IBLOCKS) + (2 * kb + s - 1))
                        for r in range(GTILES):
                            last = dve.scalar_tensor_tensor(
                                V[:, kb % 2, r, :], G[:, kb % UNITS, r, s * C:(s + 1) * C],
                                wgt[:, ds(it * ITILES + (kb * GTILES + r), 1), s],
                                V[:, kb % 2, r, :], ALU.mult, ALU.add)
                        last.then_inc(corner[l] if s < 3 else blended[l], 1)

                def image(it, more, jobs=False):
                    for kb in range(IBLOCKS):
                        if more or kb + 1 < IBLOCKS:
                            blend(it, kb + 1)
                        if kb == TAPS:
                            group_stats(it, 0)
                        if jobs:
                            if kb in TURN_SUM:
                                xt_copy(TURN_SUM[kb])
                            if kb in OFF_SUM:
                                add_bias(OFF_SUM[kb])
                            if kb == POSITIONS:
                                dve.wait_ge(off_ready, (l + 1) * N)
                                positions(1, N)
                            if kb == ROWS:
                                sample_rows(1, N)
                            if kb == WEIGHTS:
                                bilinear_weights(1, N)
                            if kb == IBLOCKS - 2:
                                dve.wait_ge(wgt_ready, 2 * l + 2)
                    group_stats(it, 1)

                def group_stats(it, b):
                    dve.wait_ge(acc_cp[l], it * IGROUPS + (b + 1 + 1))
                    dve.bn_stats(stats[:, ds(it * IGROUPS + b, 1), :].rearrange("p g s -> p (g s)"),
                                 A[l][:, ds(it * HW + b * BANK, BANK)]).then_inc(acc_stats[l], 1)

                blend(0, 0)
                image(0, True, jobs=True)
                with dve.Fori(1, N - 1) as it:
                    image(it, True)
                image(N - 1, False)

                dve.wait_ge(acc_stats[l], GROUPS)
                step(dve.bn_aggr(mv[:], stats[:].rearrange("p g s -> p (g s)")))
                dve.tensor_scalar(veps, mv[:, 1:2], BN_EPS, None, ALU.add).then_inc(var_ready, 1)
                dve.wait_ge(small_in, 16 * SMALL)
                dve.wait_ge(root_ready, l + 1)
                dve.wait_ge(var_ready, l + 1)
                step(dve.reciprocal(rinv, root))
                step(dve.tensor_tensor(sq, rinv, rinv, ALU.mult))
                step(dve.tensor_tensor(corr, sq, veps, ALU.mult))
                step(dve.tensor_scalar(corr, corr, -0.5, 1.5, ALU.mult, ALU.add))
                step(dve.tensor_tensor(rinv, rinv, corr, ALU.mult))
                step(dve.tensor_tensor(bn_scale, rinv, bn[l][:, 0:1], ALU.mult))
                step(dve.tensor_tensor(mscale, mv[:, 0:1], bn_scale, ALU.mult))
                dve.tensor_tensor(bn_shift, bn[l][:, 1:2], mscale, ALU.subtract).then_inc(norm_ready, 1)

            dve.wait_ge(norm_ready, LAYERS)
            dve.wait_ge(acc_cp[1], GROUPS + 1)

            def add_residual(n):
                for half in range(2):
                    own = slice(n * HW + half * BANK, n * HW + (half + 1) * BANK)
                    dve.scalar_tensor_tensor(F[:, own], F[:, own], bn_scale, X[:, own], ALU.mult,
                                             ALU.add).then_inc(res_add, 1)

            def take_high(n, j):
                dve.wait_ge(part_cast, 4 * n + j + 1)
                dve.scalar_tensor_tensor(resid[:, j, :], parts[:, j, :], cols[:, 2 + j:3 + j], qk32[:, j, :],
                                         ALU.mult, ALU.add).then_inc(resid_ready, 1)

            def take_middle(n, j):
                dve.wait_ge(part_cast, 4 * n + 2 + j + 1)
                dve.scalar_tensor_tensor(stacks[0:STACK, n, j, :], parts[:, j, :], cols[:, 4 + j:5 + j],
                                         resid[:, j, :], ALU.mult, ALU.add).then_inc(stack_ready, 1)

            def key_max(n, t):
                dve.wait_ge(keymax_full, n * (TS + 1) + t + 1)
                dve.tensor_reduce(nmax[:, n, t:t + 1], keymax_pair(n, t)[:], axis=AX.X, op=ALU.max,
                                  negate=True).then_inc(keymax_free, 1)

            def split_max(n):
                dve.wait_ge(keymax_free, n * TS + TS)
                b = n % 2
                step(dve.tensor_copy(nmax_p[:, b, 0, :], nmax[:, n, :]))
                step(dve.tensor_tensor(nmax_r[:, b, :], nmax[:, n, :], nmax_p[:, b, 0, :], ALU.subtract))
                step(dve.tensor_copy(nmax_p[:, b, 1, :], nmax_r[:, b, :]))
                dve.tensor_tensor(nmax_p[:, b, 2, :], nmax_r[:, b, :], nmax_p[:, b, 1, :],
                                  ALU.subtract).then_inc(max_split, 1)

            def normalise(n):
                dve.wait_ge(weighed, (n + 1) * TS)
                if n:
                    dve.wait_ge(misc_full, JOB["y", n - 1, 1] + 1)
                for t in range(TS):
                    acc = out_acc[t // 3][:, (t % 3) * (C + 1):(t % 3 + 1) * (C + 1)]
                    dve.reciprocal(einv[:, n, t:t + 1], acc[:, C:C + 1]).then_inc(einv_ready, 1)
                for t in range(TS):
                    acc = out_acc[t // 3][:, (t % 3) * (C + 1):(t % 3 + 1) * (C + 1)]
                    dve.wait_ge(einv_ready, n * TS + t + 1)
                    dve.tensor_scalar(yT[:, t, :], acc[:, 0:C], einv[:, n, t:t + 1], rowb[:, GAM:GAM + 1],
                                      ALU.mult, ALU.mult).then_inc(y_ready, 1)

            def misc_copy(job):
                what, n, half = job
                if what == "v":
                    dve.wait_ge(misc_full, JOB[job] + 1)
                    dve.tensor_tensor(vT[:, n, 4 * half:4 * half + 4, 0:C],
                                      job_bank(job).rearrange("p (t c) -> p t c", c=C),
                                      rowb[:, BV:BV + C].unsqueeze(1).broadcast_to([P, 4, C]),
                                      ALU.add).then_inc(misc_free if n else first_v, 1)
                if what == "y":
                    dve.wait_ge(misc_full, JOB[job] + 1)
                    if n:
                        dve.wait_ge(out_dma[half], 16 * n)
                    dve.tensor_tensor(OUT[:, half, :], misc[:], F[:, n * HW + half * BANK:n * HW + (half + 1) * BANK],
                                      ALU.add).then_inc(out_ready, 1)
                    dve.wait_ge(out_ready, 2 * n + half + 1)
                    dve.sem_inc(misc_free, 1)

            add_residual(0)
            add_residual(1)
            for job in FIRST_JOBS:
                misc_copy(job)
                if job[0] == "k":
                    take_high(0, job[2])
            take_middle(0, 0)
            take_middle(0, 1)
            for s in SLOTS:
                for at in range(TS):
                    if s >= 1 and at == 0:
                        normalise(s - 1)
                    if s + 1 < N:
                        for t in slot_max(s, at):
                            key_max(s + 1, t)
                        if at == split_step(s):
                            split_max(s + 1)
                    for job in misc_jobs(s, at):
                        misc_copy(job)
                    if s + 2 < N:
                        if at in (2, 3):
                            take_high(s + 2, at - 2)
                        if at in (4, 5):
                            take_middle(s + 2, at - 4)
                    if s + 3 < N and at == 4:
                        add_residual(s + 3)
            normalise(N - 1)
            for job in LAST_JOBS:
                misc_copy(job)

        @block.tensor
        def _(pe):
            def transposes(bank_cols, tiles):
                for j, tile in enumerate(tiles):
                    last = pe.transpose(bank_cols[:, j * P:(j + 1) * P], tile, ident)
                return last

            def warm_up(count):
                for _ in range(count):
                    pe.matmul(bank[0][:], zeros[:, 0:P], zeros[:], start=True, stop=True)

            pe.wait_ge(consts_dve, 1)
            warm_up(2)
            pe.wait_ge(consts, CONSTS)
            for l in range(LAYERS):
                def turn_input(n, half):
                    if l * N + n:
                        pe.wait_ge((xt_dve, xt_act)[half], l * N + n)
                    transposes(xt_acc[half], [tile_cols(l, n, 4 * half + j) for j in range(4)]).then_inc(xt_pe, 1)

                def image_in(n):
                    if l == 0:
                        pe.wait_ge(x_in[n], 16)
                    else:
                        pe.wait_ge(xn_ready, n + 1)

                def products(n, half):
                    if half == 0:
                        image_in(n)
                        if l * N + n:
                            pe.wait_ge(z_act, l * N + n)
                    for t in range(4 * half, 4 * half + 4):
                        last = pe.matmul(z_acc[:, t * TAPS * NOFF:(t + 1) * TAPS * NOFF], tile_cols(l, n, t),
                                         off_T[l][:], start=True, stop=True)
                    if half:
                        last.then_inc(z_pe, 1)

                def sum_x(n):
                    pe.wait_ge(z_act, l * N + n + 1)
                    if l * N + n:
                        pe.wait_ge(off_ready, l * N + n)
                    for j in range(KH):
                        last = pe.matmul(u_acc, band[:, j, REACH:REACH + P], ZS[:, j, :, :].rearrange("p t j -> p (t j)"),
                                         start=(j == 0), stop=(j == KH - 1))
                    last.then_inc(u_pe, 1)

                def sum_y(n):
                    pe.wait_ge(u_act, l * N + n + 1)
                    moves = [(0, 0, 0), (-1, -W, 0), (1, W, 0), (-1, P - W, -1), (1, W - P, 1)]
                    for j, (dy, by, other) in enumerate(moves):
                        t0, t1 = max(0, -other), TS - max(0, other)
                        last = pe.matmul(off_acc.rearrange("p (t j) -> p t j", j=NOFF)[:, t0:t1, :],
                                         band[:, 1, REACH + by:REACH + by + P], US[:, t0 + other:t1 + other, dy + 1, :],
                                         start=(j == 0), stop=(j == len(moves) - 1))
                    last.then_inc(off_pe, 1)

                def setup(i):
                    if i:
                        pe.wait_ge(setup_cp, i)
                    if i in (0, SETUPS - 1):
                        m = min(i, 1)
                        pe.wait_ge(offw_in[m], 16 * 2)
                        w = off_nat[m][:].rearrange("o (c y x) -> o x y c", x=KH, y=KH)
                        for k in range(TAPS):
                            pe.transpose(setup_acc[:, k * NOFF:(k + 1) * NOFF], w[:, k // KH, k % KH, :],
                                         ident[0:NOFF, 0:NOFF])
                    if i == 0:
                        pe.wait_ge(bias_in, 16 * 2)
                        pe.wait_ge(consts_dve, 2)
                        last = pe.matmul(setup_acc[:, 128:128 + NOFF], ones[:], row[:, 0:NOFF], start=True, stop=True)
                    elif i < SETUPS - 1:
                        m, third = divmod(i - 1, 3)
                        pe.wait_ge(dcnw_in[m], 16)
                        w = dcn_nat[m][:].rearrange("o (c k) -> o k c", k=TAPS)
                        last = transposes(setup_acc, [w[:, k, :] for k in range(*(0, 4, 8, 9)[third:third + 2])])
                    else:
                        pe.wait_ge(small_in, 16 * SMALL)
                        pe.wait_ge(consts_dve, 2 + MASKS)
                        for j in range(6):
                            pe.matmul(setup_acc[0:STACK, 60 + j:61 + j], cols_row[:, j, :], ones[:, 0:1],
                                      start=True, stop=True)
                        pe.matmul(setup_acc[:, 128:128 + ROWLEN - NOFF], ones[:], row[:, NOFF:ROWLEN],
                                  start=True, stop=True)
                        pe.transpose(setup_acc[:, 320:320 + D], qkv_nat[0:D, 0, :], ident[0:D, 0:D])
                        pe.transpose(setup_acc[:, 352:352 + D], qkv_nat[0:D, 1, :], ident[0:D, 0:D])
                        last = pe.transpose(setup_acc[:, 384:512], qkv_nat[:, 2, :], ident)
                    last.then_inc(setup_pe, 1)

                if l == 0:
                    image_in(0)
                    turn_input(0, 0)
                    turn_input(0, 1)
                    setup(0)
                    pe.wait_ge(setup_cp, 1)
                    products(0, 0)
                    products(0, 1)
                    sum_x(0)
                    sum_y(0)
                    for i in range(1, 4):
                        setup(i)
                else:
                    products(0, 0)
                    products(0, 1)
                    turn_input(0, 0)
                    sum_x(0)
                    turn_input(0, 1)
                    sum_y(0)

                def turn(it, kb):
                    pe.wait_ge(blended[l], it * IBLOCKS + (kb + 1 + G_CREDIT))
                    pe.wait_ge(turned_cp[l], it * IBLOCKS + (kb + 1))
                    transposes(bank[kb % 2], [V[:, kb % 2, r, :] for r in range(GTILES)]).then_inc(turned[l], 1)

                def image(it, more, jobs=False):
                    for kb in range(IBLOCKS):
                        if jobs:
                            if kb in OFF_SUM:
                                sum_y(OFF_SUM[kb])
                            if kb in Z_FIRST:
                                products(Z_FIRST[kb], 0)
                            if kb in Z_SECOND:
                                products(Z_SECOND[kb], 1)
                            if kb in TURN_SUM:
                                turn_input(TURN_SUM[kb], 0)
                                turn_input(TURN_SUM[kb], 1)
                                sum_x(TURN_SUM[kb])
                            if l == 0 and kb in LATE_SETUP:
                                setup(LATE_SETUP[kb])
                        k = kb % TAPS
                        turn_next = more or kb + 1 < IBLOCKS
                        if turn_next and k < TAPS - 1:
                            turn(it, kb + 1)
                        if k == 0:
                            pe.wait_ge(acc_cp[l], it * IGROUPS + (kb // TAPS + 1))
                        pe.wait_ge(turned_cp[l], it * IBLOCKS + (kb + 1 + CREDIT))
                        pe.matmul(conv_acc, dcn_T[l][:, k, :], CT[:, kb % 2, :], start=(k == 0),
                                  stop=(k == TAPS - 1)).then_inc(conv_mm[l], 1)
                        if turn_next and k == TAPS - 1:
                            turn(it, kb + 1)

                turn(0, 0)
                if l == 0:
                    pe.wait_ge(setup_cp, 4)
                image(0, True, jobs=True)
                with pe.Fori(1, N - 1) as it:
                    image(it, True)
                image(N - 1, False)
                warm_up(4)

            pe.wait_ge(turned_cp[1], CREDIT + GROUPS * TAPS)
            pe.wait_ge(acc_cp[1], GROUPS + 1)
            pe.wait_ge(identb_ready, 1)

            def misc_job(job):
                what, n, half = job
                to = job_bank(job)
                if misc_uses(job) > 0:
                    pe.wait_ge(misc_free, misc_uses(job))
                if what in "qk":
                    pe.wait_ge(f_ready, 2 * n + half + 1)
                    last = pe.matmul(to[0:STACK], qk_T[:, "qk".index(what), :],
                                     F[:, n * HW + half * BANK:n * HW + (half + 1) * BANK], start=True, stop=True)
                elif what == "v":
                    for j in range(4):
                        at = n * HW + (4 * half + j) * P
                        last = pe.matmul(to[:, j * P:(j + 1) * P], F[:, at:at + P], wv_T[:], start=True, stop=True)
                else:
                    pe.wait_ge(y_ready, n * TS + 4 * half + 4)
                    last = transposes(to, [yT[:, 4 * half + j, :] for j in range(4)])
                last.then_inc(misc_full, 1)

            def key_scores(n, t):
                use = n * (TS + 1) + t
                if t == 0:
                    pe.wait_ge(stack_ready, 2 * n + 2)
                    if n:
                        pe.wait_ge(stack_full, n)
                elif n:
                    pe.wait_ge(keymax_free, n * TS + t)
                elif t > 1:
                    pe.wait_ge(keymax_free, t - 1)
                for half in range(2):
                    last = pe.matmul(keymax_pair(n, t)[:, half * BANK:(half + 1) * BANK],
                                     stacks[0:STACK, n, 1, t * P:(t + 1) * P],
                                     stacks[0:STACK, n, 0, half * BANK:(half + 1) * BANK], start=True, stop=True)
                last.then_inc(keymax_full, 1)

            def max_rows(n):
                pe.wait_ge(max_split, n + 1)
                for t in range(TS):
                    last = pe.matmul(pair[0][STACK:KROWS, t * P:(t + 1) * P], nmax_p[:, n % 2, :, t], identb[:],
                                     start=True, stop=True)
                last.then_inc(keymax_full, 1)

            def scores(n, j):
                i = n * TS + j
                if j == 0:
                    pe.wait_ge(stack_full, n + 1)
                    pe.wait_ge(ones_ready, 2)
                if i:
                    pe.wait_ge(expd, i)
                for half in range(2):
                    last = pe.matmul(pair[1][:, half * BANK:(half + 1) * BANK],
                                     stacks[0:KROWS, n, 0, j * P:(j + 1) * P],
                                     stacks[0:KROWS, n, 1, half * BANK:(half + 1) * BANK], start=True, stop=True)
                last.then_inc(score_full, 1)

            def weigh(n, j):
                pe.wait_ge(expd, n * TS + j + 1)
                if n == 0 and j == 0:
                    pe.wait_ge(first_v, 2)
                for t in range(TS):
                    if n and j == 0:
                        pe.wait_ge(y_ready, min((n - 1) * TS + (t // 3 + 1) * 3, n * TS))
                    last = pe.matmul(out_acc[t // 3][:, (t % 3) * (C + 1):(t % 3 + 1) * (C + 1)],
                                     probs[:, (n * TS + j) % PRING, t * P:(t + 1) * P], vT[:, n, j, :],
                                     start=(j == 0 and t % 3 == 0), stop=(j == TS - 1), skip_group_check=True)
                last.then_inc(weighed, 1)

            for job in FIRST_JOBS:
                misc_job(job)
            for s in SLOTS:
                for step in range(TS):
                    late = ()
                    if s + 1 < N:
                        first, *late = slot_max(s, step) or (None,)
                        if first is not None:
                            key_scores(s + 1, first)
                        if step == split_step(s) + 1:
                            max_rows(s + 1)
                    if s >= 0 and step + 1 < TS:
                        scores(s, step + 1)
                    if s + 1 < N and step + 1 == TS:
                        scores(s + 1, 0)
                    if s >= 0:
                        weigh(s, step)
                    for t in late:
                        key_scores(s + 1, t)
                    for job in misc_jobs(s, step):
                        misc_job(job)
            for job in LAST_JOBS:
                misc_job(job)


_LAYER = ['tm{}_w', 'tm{}_b', 'tr{}_w', 'tr{}_b', 'dcn{}_w', 'bn{}_g', 'bn{}_b']
_ATTN = ['wq', 'bq', 'wk', 'bk', 'wv', 'bv', 'gamma']


def kernel(**inputs):
    import numpy as _np
    import concourse.bacc as _bacc
    from concourse import mybir as _mybir
    from concourse.bass_utils import run_bass_kernel_spmd as _run

    nc = _bacc.Bacc("TRN2", target_bir_lowering=False, num_devices=1)
    arrays = {}

    def dram(name):
        a = _np.ascontiguousarray(inputs[name])
        if a.ndim == 0:
            a = a.reshape(1)
        arrays[f"in_{name}_dram"] = a
        return nc.dram_tensor(f"in_{name}_dram", a.shape, _mybir.dt.from_np(a.dtype), kind="ExternalInput").ap()

    x = dram("x")
    layers = [[dram("L0_conv_" + name.format(l)) for l in (1, 2)] for name in _LAYER]
    attn = [dram("L1_conv_" + name) for name in _ATTN]
    n, c, h, w = inputs["x"].shape
    out = nc.dram_tensor("out_0_dram", (n, c, h, w), _mybir.dt.float32, kind="ExternalOutput").ap()
    tables = [nc.dram_tensor(f"table{i}", [images * h * w + w + 1, 4 * c], _mybir.dt.float32)
              for i, images in enumerate((1, n - 1))]
    deform_resblock_attention(nc, x, *layers, *attn, out, tables)
    r = _run(nc, [arrays], core_ids=[0])
    return r.results[0]["out_0_dram"]
```

```python
import concourse.bass as bass
from concourse import mybir
from contextlib import ExitStack


def deform_resblock_attention(nc, x, tm_w, tm_b, tr_w, tr_b, dcn_w, bn_g, bn_b,
                              wq, bq, wk, bk, wv, bv, gamma, out, tables):
    f32, i32, bf16 = mybir.dt.float32, mybir.dt.int32, mybir.dt.bfloat16
    ALU, ACT, AX = mybir.AluOpType, mybir.ActivationFunctionType, mybir.AxisListType
    ds = bass.ds

    N, C, H, W = x.shape
    HW = H * W
    PIX = N * HW
    P = 128
    assert N * W == P and C == P
    KH = 3
    TAPS = KH * KH
    NOFF = 6
    BANK = 512
    TS = HW // P
    TROWS = P // W
    GTILES = BANK // P
    IGROUPS = TS // GTILES
    GROUPS = N * IGROUPS
    GT = TAPS * GTILES
    ITILES = IGROUPS * GT
    TILES = GROUPS * GT
    DENSE_TAP = TAPS // 2
    GATHER_TAPS = [k for k in range(TAPS) if k != DENSE_TAP]
    GBLOCKS = len(GATHER_TAPS)
    IBLOCKS = IGROUPS * GBLOCKS
    DTILES = IGROUPS * GTILES
    CORNERS = [(0, 0), (0, 1), (1, 0), (1, 1)]
    UNITS = 4
    V_RING = 4
    ROUND = 12582912.0
    REACH = P - W
    BN_EPS = 1e-5
    D = wq.shape[0]
    LAYERS = 2
    BV = LAYERS * NOFF
    GAM = BV + C
    ROWLEN = GAM + 1
    Q_PARTS = "hhmmhl"
    K_PARTS = "hmhmlh"
    STACK = len(Q_PARTS) * D
    KROWS = STACK + 3

    with ExitStack() as ctx:
        def sb(name, shape, dt=f32):
            return ctx.enter_context(nc.sbuf_tensor(name, shape, dt))

        def sem(name):
            return ctx.enter_context(nc.semaphore(name))

        X = sb("X", [P, PIX])
        A = [sb(f"A{l}", [P, PIX]) for l in range(LAYERS)]
        XN = [X, A[1]]
        XT = sb("XT", [P, PIX // P, C])
        ZS = sb("ZS", [P, KH, TS, KH * NOFF])
        US = sb("US", [P, TS, KH, NOFF])
        OFT = sb("OFT", [P, N, TS, NOFF])
        band = sb("band", [P, KH, 2 * REACH + P])
        ident = band[:, 1, REACH:REACH + P]
        identb = sb("identb", [P, P], bf16)
        zeros = sb("zeros", [P, 4 * C])
        ones = sb("ones", [1, P])
        grid_i = sb("grid_i", [P, 2], i32)
        gridw = sb("gridw", [P, 1])
        gridr = sb("gridr", [P, 1])
        tile_i = sb("tile_i", [P, TS], i32)
        gridh = sb("gridh", [P, TS])
        base = sb("base", [P, 2, N * TS])
        rowpos = sb("rowpos", [P, 2, KH, N * TS])
        pos = sb("pos", [P, 2, TILES])
        low = sb("low", [P, 2, TILES])
        dist = sb("dist", [P, 2, 2, TILES])
        hat = sb("hat", [P, 2, 2, TILES])
        wgt = sb("wgt", [P, TILES, 4])
        rowf = sb("rowf", [P, TILES])
        rowi = sb("rowi", [P, TILES], i32)
        rows_now = sb("rows_now", [P, IGROUPS, GT], i32)
        G = sb("G", [P, UNITS, GTILES, 4 * C])
        grid_wi = sb("grid_wi", [P, W], i32)
        grid_w = sb("grid_w", [P, W])
        dhat = sb("dhat", [P, 2, GTILES, W])
        S = sb("S", [P, 2, H, W])
        ST = sb("ST", [P, 2, TS * P])
        XS = sb("XS", [P, TS, C])
        CTD = sb("CTD", [P, BANK])
        V = sb("V", [P, V_RING, GTILES, C])
        CT = sb("CT", [P, 2, BANK])
        dcn_T = [sb(f"dcn_T{l}", [P, TAPS, P]) for l in range(LAYERS)]
        off_nat = [sb(f"off_nat{l}", [NOFF, C * TAPS]) for l in range(LAYERS)]
        off_T = [sb(f"off_T{l}", [P, TAPS * NOFF]) for l in range(LAYERS)]
        row = sb("row", [1, ROWLEN])
        rowb = sb("rowb", [P, ROWLEN])
        bn = [sb(f"bn{l}", [P, 2]) for l in range(LAYERS)]
        stats = sb("stats", [P, GROUPS, 6])
        mv = sb("mv", [P, 2])
        nrm = sb("nrm", [P, 8])
        veps = nrm[:, 0:1]
        root = nrm[:, 1:2]
        rinv = nrm[:, 2:3]
        sq = nrm[:, 3:4]
        corr = nrm[:, 4:5]
        bn_scale = nrm[:, 5:6]
        mscale = nrm[:, 6:7]
        bn_shift = nrm[:, 7:8]
        warm = sb("warm", [1, 1])
        qkv_nat = sb("qkv_nat", [P, 3, C])
        qk_T = sb("qk_T", [P, 2, STACK])
        wv_T = sb("wv_T", [P, C])
        cols_row = sb("cols_row", [1, 6, STACK])
        cols = sb("cols", [STACK, 6])
        nmax = sb("nmax", [P, N, TS])
        nmax_r = sb("nmax_r", [P, 2, TS])
        nmax_p = sb("nmax_p", [P, 2, 3, TS], bf16)
        einv = sb("einv", [P, N, TS])
        stacks = sb("stacks", [P, N, 2, HW], bf16)
        yT = sb("yT", [P, TS, C])
        dcn_nat = [stacks[:].rearrange("p n b k -> p (n b k)").bitcast(f32)[:, l * C * TAPS:(l + 1) * C * TAPS]
                   for l in range(LAYERS)]
        F = A[1]
        probs = A[0][:].rearrange("p (r k) -> p r k", r=4)
        PRING = 4
        qk32 = XT[0:STACK, 0:2 * TS, :].rearrange("p (b t) k -> p b (t k)", b=2)
        resid = XT[0:STACK, 2 * TS:4 * TS, :].rearrange("p (b t) k -> p b (t k)", b=2)
        gflat = G[:].rearrange("p a b c -> p (a b c)")
        vT = gflat[:, 0:N * TS * (C + 1)].rearrange("p (n t c) -> p n t c", n=N, t=TS)
        parts = gflat[0:STACK, 5 * HW:6 * HW].bitcast(bf16).rearrange("p (b k) -> p b k", b=2)
        OUT = gflat[:, 6 * HW:7 * HW].rearrange("p (b k) -> p b k", b=2)

        bank = [ctx.enter_context(nc.psum_tensor(f"bank{i}", [P, BANK], f32))[:] for i in range(2)]
        pair = [ctx.enter_context(nc.psum_tensor(f"pair{i}", [P, 2 * BANK], f32)) for i in range(3)]
        bank += [pair[2][:, 0:BANK], pair[2][:, BANK:2 * BANK]]
        out_acc = bank[0:3]
        misc = bank[3]
        xt_acc = bank[2:4]
        conv_acc = pair[0][:, 0:BANK]
        dense_acc = pair[0][:, BANK:2 * BANK]
        z_acc = pair[1][:, 0:TS * TAPS * NOFF]
        u_acc = pair[1][:, BANK:BANK + TS * KH * NOFF]
        off_acc = pair[1][:, BANK + TS * KH * NOFF:BANK + TS * (KH + 1) * NOFF]

        x_in = [sem(f"x_in{n}") for n in range(N)]
        offw_in = [sem(f"offw_in{l}") for l in range(LAYERS)]
        bias_in = sem("bias_in")
        dcnw_in = [sem(f"dcnw_in{m}") for m in range(LAYERS)]
        small_in = sem("small_in")
        consts = sem("consts")
        hat_step = [sem(f"hat_step{l}") for l in range(LAYERS)]
        s_ready = [sem(f"s_ready{l}") for l in range(LAYERS)]
        s_turned = [sem(f"s_turned{l}") for l in range(LAYERS)]
        st_ready = [sem(f"st_ready{l}") for l in range(LAYERS)]
        xs_ready = [sem(f"xs_ready{l}") for l in range(LAYERS)]
        dense_mm = [sem(f"dense_mm{l}") for l in range(LAYERS)]
        dense_cp = [sem(f"dense_cp{l}") for l in range(LAYERS)]
        consts_dve = sem("consts_dve")
        identb_ready = sem("identb_ready")
        fill_out = sem("fill_out")
        setup_pe = sem("setup_pe")
        setup_cp = sem("setup_cp")
        xt_pe = sem("xt_pe")
        xt_dve = sem("xt_dve")
        xt_act = sem("xt_act")
        z_pe = sem("z_pe")
        z_act = sem("z_act")
        u_pe = sem("u_pe")
        u_act = sem("u_act")
        off_pe = sem("off_pe")
        off_ready = sem("off_ready")
        dve_step = sem("dve_step")
        rows_ready = sem("rows_ready")
        wgt_ready = sem("wgt_ready")
        table_out = [[sem(f"table_out{l}_{n}") for n in range(N)] for l in range(LAYERS)]
        rows_copied = sem("rows_copied")
        gathered = [[sem(f"gathered{l}_{u}") for u in range(UNITS)] for l in range(LAYERS)]
        scaled = [sem(f"scaled{l}") for l in range(LAYERS)]
        corner = [sem(f"corner{l}") for l in range(LAYERS)]
        blended = [sem(f"blended{l}") for l in range(LAYERS)]
        turned = [sem(f"turned{l}") for l in range(LAYERS)]
        turned_cp = [sem(f"turned_cp{l}") for l in range(LAYERS)]
        conv_mm = [sem(f"conv_mm{l}") for l in range(LAYERS)]
        acc_cp = [sem(f"acc_cp{l}") for l in range(LAYERS)]
        acc_stats = [sem(f"acc_stats{l}") for l in range(LAYERS)]
        var_ready = sem("var_ready")
        root_ready = sem("root_ready")
        norm_ready = sem("norm_ready")
        xn_ready = sem("xn_ready")
        res_add = sem("res_add")
        f_ready = sem("f_ready")
        ones_ready = sem("ones_ready")
        misc_full = sem("misc_full")
        misc_free = sem("misc_free")
        first_v = sem("first_v")
        qk_cp = sem("qk_cp")
        part_cast = sem("part_cast")
        resid_ready = sem("resid_ready")
        stack_ready = sem("stack_ready")
        keymax_full = sem("keymax_full")
        keymax_free = sem("keymax_free")
        score_full = sem("score_full")
        max_split = sem("max_split")
        stack_full = sem("stack_full")
        expd = sem("expd")
        weighed = sem("weighed")
        einv_ready = sem("einv_ready")
        y_ready = sem("y_ready")
        y_act = sem("y_act")
        out_ready = sem("out_ready")
        out_dma = [sem(f"out_dma{i}") for i in range(2)]

        G_CREDIT = UNITS
        CREDIT = 2
        CONSTS = 1 + KH + 5
        SMALL = 2 * LAYERS + 9
        TABLE_AT = [0] + [(n - 1) * HW for n in range(1, N)]
        FILLS = 2 * 2
        MASKS = sum(p != "h" for p in Q_PARTS + K_PARTS) + (Q_PARTS + K_PARTS).count("l")

        def tile_cols(l, n, t):
            return XN[l][:, n * HW + t * P:n * HW + (t + 1) * P]

        AHEAD = 2
        START = {n: 4 * (n - AHEAD) for n in range(AHEAD, N)}
        Z_FIRST = {START[n]: n for n in START}
        Z_SECOND = {START[n] + 1: n for n in START}
        TURN_SUM = {START[n] + 2: n for n in START}
        OFF_SUM = {START[n] + 3: n for n in START}
        RELU = {START[n] - 2: n for n in START}
        POSITIONS = START[N - 1] + 5
        WEIGHTS = {6: 1, 13: 2, 14: 3}
        LATE_SETUP = {START[N - 1] + 4 + i: 4 + i for i in range(4)}
        SETUPS = 8
        assert max(LATE_SETUP) < IBLOCKS and min(WEIGHTS) < IBLOCKS - 2 and max(WEIGHTS) < IBLOCKS

        MAKE_S = {0: 0, 2: 1, 3: 2, 4: 3}
        TURN_S = {g + 1: j for g, j in MAKE_S.items()}
        USE_S = {g + 2: j for g, j in MAKE_S.items()}
        assert max(USE_S) < GBLOCKS
        assert not any(kb % GBLOCKS in TURN_S for kb in TURN_SUM)

        def dense_tile(it, b, j):
            return it * DTILES + (b * GTILES + j)

        def dense_turned(kb):
            return sum(1 for i in range(kb) if i % GBLOCKS in TURN_S)

        def images_turned(kb):
            return AHEAD + sum(1 for i in TURN_SUM if i < kb)

        def setup_acc(i):
            return pair[0][:, BANK:2 * BANK] if i < 4 else pair[1][:, BANK:2 * BANK]

        def block_tile(kb):
            return kb // GBLOCKS * GT + GATHER_TAPS[kb % GBLOCKS] * GTILES

        SLOTS = range(-1, N)
        SLOT_MAX = {0: (0, 1), 1: (2, 3), 2: (4,), 3: (5,), 4: (6,), 5: (7,)}
        FIRST_MAX = {0: (0, 1), 1: (2, 3), 2: (4, 5), 3: (6, 7)}
        SECOND_MAX = {0: (0,), 1: (1, 2), 2: (3,), 3: (4, 5), 4: (6,), 5: (7,)}
        FIRST_MISC = {i: (job,) for i, job in enumerate((("q", 0), ("q", 1), ("k", 0), ("k", 1)))}
        SLOT_MISC = {0: (("q", 0), ("q", 1)), 1: (("k", 0),), 2: (("k", 1),), 3: (("y", 0),),
                     4: (("y", 1),), 5: (("v", 0),), 6: (("v", 1),)}

        MAX_BY_SLOT = {-1: FIRST_MAX, 0: SECOND_MAX}

        def slot_max(s, step):
            return MAX_BY_SLOT.get(s, SLOT_MAX).get(step, ())

        def split_step(s):
            return max(MAX_BY_SLOT.get(s, SLOT_MAX))

        def next_scores(s):
            return split_step(s) + 2 if s < 0 else TS - 1

        def misc_jobs(s, step):
            for what, half in (FIRST_MISC if s < 0 else SLOT_MISC).get(step, ()):
                n = s + {"q": 2, "k": 2, "v": 1, "y": -1}[what]
                if 0 <= n < N and (what != "v" or s >= 0):
                    yield what, n, half

        FIRST_JOBS = [(what, 0, half) for what in "qkv" for half in range(2)]
        LAST_JOBS = [("y", N - 1, half) for half in range(2)]
        JOBS = FIRST_JOBS + [j for s in SLOTS for step in range(TS) for j in misc_jobs(s, step)] + LAST_JOBS
        JOB = {job: i for i, job in enumerate(JOBS)}
        OWN_BANK = {}
        for half in range(2):
            OWN_BANK["q", 0, half] = pair[1][:, half * BANK:(half + 1) * BANK]
            OWN_BANK["k", 0, half] = pair[0][:, half * BANK:(half + 1) * BANK]
            OWN_BANK["v", 0, half] = out_acc[half][:]
        for what in "qk":
            OWN_BANK[what, 1, 0] = out_acc[2][:]
        OWN_BANK["y", N - 1, 1] = pair[1][:, 0:BANK]

        def job_bank(job):
            return OWN_BANK[job] if job in OWN_BANK else misc[:]

        def misc_uses(job):
            uses = JOB[job] - len(FIRST_JOBS)
            return uses - 1 if uses < 4 or job == LAST_JOBS[1] else uses

        YD = 2 * 3

        def out_tile(t):
            return out_acc[t // 3][:, (t % 3) * (C + 1):(t % 3 + 1) * (C + 1)]

        def keymax_pair(n, t):
            return pair[t % 2 if n == 0 else 0]

        block = ctx.enter_context(nc.Block())

        @block.sync
        def _(sp):
            def load_image(n):
                sp.dma_start(X[:, n * HW:(n + 1) * HW], x[n].rearrange("c h w -> c (h w)")).then_inc(x_in[n], 16)

            def load_dcn(m):
                sp.dma_start(dcn_nat[m][:], dcn_w[m].rearrange("o c i j -> o (c i j)")).then_inc(dcnw_in[m], 16)

            def write_table(l, n):
                sp.wait_ge(xt_dve, l * N + n + 1)
                sp.wait_ge(xt_act, l * N + n + 1)
                for s, (dy, dx) in enumerate(CORNERS):
                    first = TABLE_AT[n] + W + 1 - (dy * W + dx)
                    sp.dma_start(tables[min(n, 1)][first:first + HW, s * C:(s + 1) * C].rearrange("(t p) c -> p t c", p=P),
                                 XT[:, n * TS:(n + 1) * TS, :]).then_inc(table_out[l][n], 16)

            load_image(0)
            sp.wait_ge(consts_dve, 1)
            for table in tables:
                sp.dma_start(table[0:W + 1, :], zeros[0:W + 1, :]).then_inc(fill_out, 16)
                end = table.shape[0]
                sp.dma_start(table[end - W - 1:end, :], zeros[0:W + 1, :]).then_inc(fill_out, 16)
            load_dcn(0)
            load_image(1)
            sp.wait_ge(fill_out, 16 * FILLS)
            write_table(0, 0)
            load_image(2)
            load_image(3)
            load_dcn(1)
            sp.dma_start(off_nat[1][0:4, :], tm_w[1].rearrange("o c i j -> o (c i j)")).then_inc(offw_in[1], 16)
            sp.dma_start(off_nat[1][4:6, :], tr_w[1].rearrange("o c i j -> o (c i j)")).then_inc(offw_in[1], 16)
            sp.dma_start(row[:, NOFF:NOFF + 4], tm_b[1].rearrange("(a n) -> a n", a=1)).then_inc(small_in, 16)
            sp.dma_start(row[:, NOFF + 4:NOFF + 6], tr_b[1].rearrange("(a n) -> a n", a=1)).then_inc(small_in, 16)
            for m in range(LAYERS):
                sp.dma_start(bn[m][:, 0:1], bn_g[m].rearrange("(n a) -> n a", a=1)).then_inc(small_in, 16)
                sp.dma_start(bn[m][:, 1:2], bn_b[m].rearrange("(n a) -> n a", a=1)).then_inc(small_in, 16)
            sp.dma_start(row[:, BV:BV + C], bv.rearrange("(a n) -> a n", a=1)).then_inc(small_in, 16)
            sp.dma_start(row[:, GAM:GAM + 1], gamma.rearrange("(a n) -> a n", a=1)).then_inc(small_in, 16)
            for j, b in enumerate((bq, bk)):
                sp.dma_start(cols_row[:, j, :].rearrange("a (b d) -> a b d", d=D),
                             b.rearrange("(a u d) -> a u d", a=1, u=1)
                             .broadcast_to([1, len(Q_PARTS), D])).then_inc(small_in, 16)
            for j, w in enumerate((wq, wk, wv)):
                sp.dma_start(qkv_nat[0:w.shape[0], j, :], w).then_inc(small_in, 16)
            for n in range(1, N):
                write_table(0, n)
            sp.wait_ge(blended[0], G_CREDIT + GROUPS * GBLOCKS)
            for n in range(N):
                write_table(1, n)
            for n in range(N):
                for half in range(2):
                    sp.wait_ge(out_ready, n * 2 + half + 1)
                    sp.dma_start(out[n].rearrange("c h w -> c (h w)")[:, half * BANK:(half + 1) * BANK],
                                 OUT[:, half, :]).then_inc(out_dma[half], 16)
            for half in range(2):
                sp.wait_ge(out_dma[half], 16 * N)

        @block.gpsimd
        def _(pool):
            pool.memset(band[:], 0.0).then_inc(consts, 1)
            pool.wait_ge(consts, 1)
            for j in range(KH):
                pool.affine_select(out=band[:, j, :], in_=band[:, j, :], compare_op=ALU.not_equal, fill=1.0,
                                   base=REACH - (j - 1), pattern=[[-1, 2 * REACH + P]],
                                   channel_multiplier=1).then_inc(consts, 1)
            pool.wait_ge(consts, 1 + KH)
            pool.memset(band[:, 0, :].rearrange("p (n w) -> p n w", w=W)[:, :, 0:1], 0.0).then_inc(consts, 1)
            pool.memset(band[:, 2, :].rearrange("p (n w) -> p n w", w=W)[:, :, W - 1:W], 0.0).then_inc(consts, 1)
            pool.iota(grid_wi[:], pattern=[[1, W]], base=0, channel_multiplier=0).then_inc(consts, 1)
            pool.iota(grid_i[:], pattern=[[0, 2]], base=0, channel_multiplier=1).then_inc(consts, 1)
            pool.iota(tile_i[:], pattern=[[TROWS, TS]], base=0, channel_multiplier=0).then_inc(consts, 1)
            pool.wait_ge(consts, CONSTS)
            pool.tensor_copy(identb[:], ident).then_inc(identb_ready, 1)
            pool.wait_ge(identb_ready, 1)
            def gather_image(l, it, table):
                for b in range(IGROUPS):
                    pool.wait_ge(blended[l], it * IBLOCKS + (b * GBLOCKS + 1))
                    pool.tensor_copy(rows_now[:, b, :], rowi[:, ds(it * ITILES + b * GT, GT)]) \
                        .then_inc(rows_copied, 1)
                    pool.wait_ge(rows_copied, it * IGROUPS + (l * GROUPS + b + 1))
                    pool.nop(nofuse=True)
                    for g, k in enumerate(GATHER_TAPS):
                        kb = b * GBLOCKS + g
                        if g:
                            pool.wait_ge(blended[l], it * IBLOCKS + (kb + 1))
                            pool.nop(nofuse=True)
                        for r in range(GTILES):
                            c = k * GTILES + r
                            pool.indirect_dma_start(
                                G[:, kb % UNITS, r, :], None, table[:, :],
                                bass.IndirectOffsetOnAxis(rows_now[:, b, c:c + 1], 0)) \
                                .then_inc(gathered[l][kb % UNITS], 16)

            for l in range(LAYERS):
                pool.wait_ge(rows_ready, 3 * l + 1)
                pool.wait_ge(fill_out, 16 * FILLS)
                pool.wait_ge(table_out[l][0], 16 * 4)
                gather_image(l, 0, tables[0])
                pool.wait_ge(rows_ready, 3 * l + 3)
                for n in range(1, N):
                    pool.wait_ge(table_out[l][n], 16 * 4)
                with pool.Fori(1, N) as it:
                    gather_image(l, it, tables[1])

            pool.wait_ge(turned_cp[1], CREDIT + GROUPS * GBLOCKS)
            pool.memset(stacks[STACK:KROWS, :, 0, :], 1.0).then_inc(ones_ready, 1)
            pool.wait_ge(ones_ready, 1)
            pool.memset(vT[:, :, :, C:C + 1], 1.0).then_inc(ones_ready, 1)
            pool.wait_ge(ones_ready, 2)

        @block.scalar
        def _(act):
            act.dma_start(off_nat[0][0:4, :], tm_w[0].rearrange("o c i j -> o (c i j)")).then_inc(offw_in[0], 16)
            act.dma_start(off_nat[0][4:6, :], tr_w[0].rearrange("o c i j -> o (c i j)")).then_inc(offw_in[0], 16)
            act.dma_start(row[:, 0:4], tm_b[0].rearrange("(a n) -> a n", a=1)).then_inc(bias_in, 16)
            act.dma_start(row[:, 4:6], tr_b[0].rearrange("(a n) -> a n", a=1)).then_inc(bias_in, 16)
            act.wait_ge(consts_dve, 2)
            act.sqrt(warm[:], ones[:, 0:1])

            for l in range(LAYERS):
                def relu_input(n):
                    if l:
                        own = slice(n * HW, (n + 1) * HW)
                        act.activation(XN[1][:, own], A[0][:, own], ACT.Relu, bias=bn_shift,
                                       scale=bn_scale).then_inc(xn_ready, 1)

                def z_copy(n):
                    act.wait_ge(z_pe, l * N + n + 1)
                    act.copy(ZS[:].rearrange("p x t j -> p t x j"),
                             z_acc.rearrange("p (t x j) -> p t x j", t=TS, x=KH)).then_inc(z_act, 1)

                def u_copy(n):
                    act.wait_ge(u_pe, l * N + n + 1)
                    act.copy(US[:].rearrange("p t y j -> p (t y j)"), u_acc).then_inc(u_act, 1)

                def xt_copy(n):
                    act.wait_ge(xt_pe, 2 * (l * N + n) + 2)
                    if l:
                        act.wait_ge(table_out[0][n], 16 * 4)
                    act.copy(XT[:, n * TS + 4:(n + 1) * TS, :], xt_acc[1][:]).then_inc(xt_act, 1)

                def setup(i):
                    act.wait_ge(setup_pe, i + 1)
                    if i == 0:
                        act.copy(off_T[0][:], setup_acc(i)[:, 0:TAPS * NOFF])
                        act.copy(rowb[:, 0:NOFF], setup_acc(i)[:, 128:128 + NOFF])
                    elif i < 7:
                        m, third = divmod(i - 1, 3)
                        k0, k1 = (0, 4, 8, 9)[third:third + 2]
                        act.copy(dcn_T[m][:, k0:k1, :].rearrange("p k o -> p (k o)"), setup_acc(i)[:, 0:(k1 - k0) * P])
                    else:
                        act.copy(off_T[1][:], setup_acc(i)[:, 0:TAPS * NOFF])
                        act.copy(rowb[:, NOFF:ROWLEN], setup_acc(i)[:, 128:128 + ROWLEN - NOFF])
                        act.copy(wv_T[:], setup_acc(i)[:, 384:512])
                        act.copy(cols[:], setup_acc(i)[0:STACK, 60:66])
                        for j in range(2):
                            at = 320 + j * 32
                            act.copy(qk_T[:, j, :].rearrange("p (b d) -> p b d", d=D),
                                     setup_acc(i)[:, at:at + D].unsqueeze(1).broadcast_to([P, len(Q_PARTS), D]))
                    act.drain().then_inc(setup_cp, 1)

                if l:
                    act.wait_ge(norm_ready, 1)
                    act.wait_ge(acc_cp[0], GROUPS + 1)
                relu_input(0)
                if l == 0:
                    xt_copy(0)
                    setup(0)
                    z_copy(0)
                    u_copy(0)
                    for i in range(1, 4):
                        setup(i)
                else:
                    xt_copy(0)
                    z_copy(0)
                    u_copy(0)
                for n in range(1, AHEAD):
                    relu_input(n)
                    xt_copy(n)
                    z_copy(n)
                    u_copy(n)
                for block_no, n in RELU.items():
                    if block_no < 0:
                        relu_input(n)

                def scale(it, kb):
                    act.wait_ge(gathered[l][kb % UNITS], it * (16 * GTILES * IBLOCKS // UNITS)
                                + 16 * GTILES * (kb // UNITS + 1))
                    act.wait_ge(turned[l], it * IBLOCKS + (kb + 1))
                    for r in range(GTILES):
                        tile = ds(it * ITILES + (block_tile(kb) + r), 1)
                        act.activation(V[:, kb % V_RING, r, :], G[:, kb % UNITS, r, 0:C], ACT.Copy,
                                       scale=wgt[:, tile, 0])
                        last = act.activation(G[:, kb % UNITS, r, 3 * C:4 * C], G[:, kb % UNITS, r, 3 * C:4 * C],
                                              ACT.Copy, scale=wgt[:, tile, 3])
                    last.then_inc(scaled[l], 1)

                def image(it, more, jobs=False):
                    for kb in range(IBLOCKS):
                        if more or kb + 2 < IBLOCKS:
                            scale(it, kb + 2)
                        act.wait_ge(turned[l], it * IBLOCKS + (kb + 1 + V_RING))
                        act.wait_ge(conv_mm[l], it * IBLOCKS + (kb + 1))
                        act.copy(CT[:, kb % 2, :], bank[kb % 2][:]).then_inc(turned_cp[l], 1)
                        b, g = divmod(kb, GBLOCKS)
                        if kb == 0:
                            if jobs:
                                act.wait_ge(xt_dve, l * N + 1)
                                act.wait_ge(xt_act, l * N + 1)
                            act.wait_ge(dense_mm[l], it * DTILES + CREDIT)
                            act.copy(XS[:], XT[:, ds(it * TS, TS), :]).then_inc(xs_ready[l], 1)
                        if g == GBLOCKS - 2:
                            act.wait_ge(dense_mm[l], it * DTILES + ((b + 1) * GTILES + CREDIT))
                            act.copy(CTD[:], dense_acc).then_inc(dense_cp[l], 1)
                        if g == GBLOCKS - 1:
                            act.wait_ge(conv_mm[l], it * IBLOCKS + (kb + 1 + CREDIT))
                            act.copy(A[l][:, ds(it * HW + b * BANK, BANK)], conv_acc).then_inc(acc_cp[l], 1)
                        if jobs:
                            if kb in Z_SECOND:
                                z_copy(Z_SECOND[kb])
                            if kb in TURN_SUM:
                                xt_copy(TURN_SUM[kb])
                                u_copy(TURN_SUM[kb])
                            if kb in RELU:
                                relu_input(RELU[kb])
                            if l == 0 and kb in LATE_SETUP:
                                setup(LATE_SETUP[kb])
                            if kb == IBLOCKS - 3:
                                act.wait_ge(wgt_ready, l * N + 2)
                        if g in TURN_S:
                            d = dense_tile(it, b, TURN_S[g])
                            act.wait_ge(s_turned[l], d + (1 + CREDIT))
                            act.wait_ge(dense_mm[l], d + 1)
                            act.copy(ST[:, TURN_S[g] % 2, :], pair[2][:]).then_inc(st_ready[l], 1)

                act.wait_ge(wgt_ready, l * N + 1)
                scale(0, 0)
                scale(0, 1)
                image(0, True, jobs=True)
                act.wait_ge(wgt_ready, (l + 1) * N)
                act.wait_ge(xt_dve, (l + 1) * N)
                act.wait_ge(xt_act, (l + 1) * N)
                with act.Fori(1, N - 1) as it:
                    image(it, True)
                image(N - 1, False)

                act.wait_ge(var_ready, l + 1)
                act.sqrt(root, veps).then_inc(root_ready, 1)

            act.activation(warm[:], ones[:, 0:1], ACT.Exp)
            act.wait_ge(norm_ready, 2)

            def relu(n):
                for half in range(2):
                    own = slice(n * HW + half * BANK, n * HW + (half + 1) * BANK)
                    act.wait_ge(res_add, 2 * n + half + 1)
                    act.activation(F[:, own], F[:, own], ACT.Relu, bias=bn_shift).then_inc(f_ready, 1)

            def misc_copy(job):
                what, n, half = job
                if what in "qk":
                    j = "qk".index(what)
                    if n:
                        act.wait_ge(stack_ready, 2 * (n - 1) + j + 1)
                    act.wait_ge(misc_full, JOB[job] + 1)
                    act.activation(qk32[:, j, half * BANK:(half + 1) * BANK], job_bank(job)[0:STACK], ACT.Identity,
                                   bias=cols[:, j:j + 1]).then_inc(qk_cp, 1)
                    if n:
                        act.wait_ge(qk_cp, 4 * n + 2 * j + half + 1)
                        act.sem_inc(misc_free, 1)

            def high(n, j):
                act.wait_ge(qk_cp, 4 * n + 2 * j + 2)
                act.copy(parts[:, j, :], qk32[:, j, :]).then_inc(part_cast, 1)

            def middle(n, j):
                act.wait_ge(resid_ready, 2 * n + j + 1)
                act.copy(parts[:, j, :], resid[:, j, :]).then_inc(part_cast, 1)

            def normalise(n):
                act.wait_ge(einv_ready, 3 * (n + 1))
                if n:
                    act.wait_ge(misc_full, JOB["y", n - 1, 1] + 1)
                for t in range(YD, TS):
                    act.activation(yT[:, t, :], out_tile(t)[:, 0:C], ACT.Copy,
                                   scale=einv[:, n, t:t + 1]).then_inc(y_act, 1)

            def exps(n, j):
                i = n * TS + j
                act.wait_ge(score_full, i + 1)
                if i >= PRING:
                    act.wait_ge(weighed, i - PRING + 1)
                act.activation(probs[:, i % PRING, :], pair[1][:], ACT.Exp).then_inc(expd, 1)

            relu(0)
            for job in FIRST_JOBS:
                misc_copy(job)
                if job[0] in "qk" and job[2] == 1:
                    high(0, "qk".index(job[0]))
            middle(0, 0)
            middle(0, 1)
            relu(1)
            for s in SLOTS:
                for step in range(TS):
                    if s >= 1 and step == 0:
                        normalise(s - 1)
                    if s >= 0 and step + 1 < TS:
                        exps(s, step + 1)
                    for job in misc_jobs(s, step):
                        misc_copy(job)
                    if s + 1 < N and step == split_step(s) + 1:
                        act.wait_ge(keymax_full, (s + 1) * (TS + 1) + TS + 1)
                        act.copy(stacks[STACK:KROWS, s + 1, 1, :], pair[0][STACK:KROWS, :]) \
                            .then_inc(stack_full, 1)
                    high_from, middle_from = (2, 6) if s < 0 else (1, 3)
                    if s + 2 < N and step in (high_from, high_from + 1):
                        high(s + 2, step - high_from)
                    if s + 2 < N and step in (middle_from, middle_from + 1):
                        middle(s + 2, step - middle_from)
                    if s + 1 < N and step == next_scores(s):
                        exps(s + 1, 0)
                    if s + 3 < N and step == 5:
                        relu(s + 3)

            normalise(N - 1)

        @block.vector
        def _(dve):
            steps = [0]

            def step(instruction):
                steps[0] += 1
                instruction.then_inc(dve_step, 1)
                dve.wait_ge(dve_step, steps[0])

            dve.memset(zeros[:], 0.0).then_inc(consts_dve, 1)
            dve.memset(ones[:], 1.0).then_inc(consts_dve, 1)
            for l in range(LAYERS):
                dve.sem_inc(blended[l], G_CREDIT)
                dve.sem_inc(turned[l], V_RING)
                for free in (turned_cp[l], conv_mm[l], s_turned[l], dense_mm[l]):
                    dve.sem_inc(free, CREDIT)
                dve.sem_inc(st_ready[l], 1)
                dve.sem_inc(s_ready[l], 1)
                dve.sem_inc(acc_cp[l], 1)

            step(dve.memset(cols_row[:, 2:6, :], 0.0))
            for j, held in enumerate((Q_PARTS, K_PARTS)):
                for b, part in enumerate(held):
                    at = slice(b * D, (b + 1) * D)
                    if part != "h":
                        dve.memset(cols_row[:, 2 + j, at], -1.0).then_inc(consts_dve, 1)
                    if part == "l":
                        dve.memset(cols_row[:, 4 + j, at], -1.0).then_inc(consts_dve, 1)

            dve.wait_ge(consts, CONSTS)
            step(dve.tensor_scalar(grid_i[:, 0:1], grid_i[:, 0:1], W - 1, None, ALU.bitwise_and))
            step(dve.tensor_scalar(grid_i[:, 1:2], grid_i[:, 1:2], W.bit_length() - 1, None,
                                   ALU.logical_shift_right))
            dve.tensor_copy(gridw[:], grid_i[:, 0:1])
            dve.tensor_copy(gridr[:], grid_i[:, 1:2])
            dve.tensor_copy(grid_w[:], grid_wi[:])
            step(dve.tensor_copy(gridh[:], tile_i[:]))
            step(dve.tensor_scalar(gridh[:], gridh[:], gridr[:], None, ALU.add))

            def tile_range(n0, n1):
                return slice(n0 * ITILES, n1 * ITILES)

            def positions(n0, n1):
                tiles = tile_range(n0, n1)
                off = OFT[:, n0:n1, :, :].rearrange("p n t j -> p j (n t)")
                cur = slice(n0 * TS, n1 * TS)
                dve.tensor_tensor(base[:, 0, cur].rearrange("p (n t) -> p n t", t=TS), OFT[:, n0:n1, :, 4],
                                  gridh[:].unsqueeze(1).broadcast_to([P, n1 - n0, TS]), ALU.add)
                step(dve.tensor_scalar(base[:, 1, cur], off[:, 5], gridw[:], None, ALU.add))
                dve.tensor_tensor(rowpos[:, :, 0, cur], base[:, :, cur], off[:, 0:4:2], ALU.subtract)
                dve.tensor_copy(rowpos[:, :, 1, cur], base[:, :, cur])
                step(dve.tensor_tensor(rowpos[:, :, 2, cur], base[:, :, cur], off[:, 0:4:2], ALU.add))
                for a in range(2):
                    src = rowpos[:, a, :, cur].rearrange("p e (g i) -> p e g i", i=GTILES)
                    cross = off[:, 2 * a + 1].rearrange("p (g i) -> p g i", i=GTILES).unsqueeze(1) \
                        .broadcast_to([P, KH, (n1 - n0) * IGROUPS, GTILES])
                    dst = pos[:, a, tiles].rearrange("p (g e d i) -> p d e g i", e=KH, d=KH, i=GTILES)
                    dve.tensor_tensor(dst[:, 0], src, cross, ALU.subtract)
                    dve.tensor_copy(dst[:, 1], src)
                    last = dve.tensor_tensor(dst[:, 2], src, cross, ALU.add)
                step(last)

            def sample_rows(n0, n1):
                tiles = tile_range(n0, n1)
                step(dve.tensor_scalar(low[:, :, tiles], pos[:, :, tiles], -0.5, 0.0, ALU.add, ALU.max))
                step(dve.tensor_scalar(low[:, :, tiles], low[:, :, tiles], float(H - 2), ROUND, ALU.min, ALU.add))
                step(dve.tensor_scalar(low[:, :, tiles], low[:, :, tiles], -ROUND, None, ALU.add))
                step(dve.scalar_tensor_tensor(rowf[:, tiles], low[:, 0, tiles], float(W), low[:, 1, tiles],
                                              ALU.mult, ALU.add))
                for n in range(n0, n1):
                    own = tile_range(n, n + 1)
                    last = dve.tensor_scalar(rowi[:, own], rowf[:, own], float(TABLE_AT[n] + W + 1), None, ALU.add)
                last.then_inc(rows_ready, 1)

            def bilinear_weights(n0, n1):
                tiles = tile_range(n0, n1)
                step(dve.tensor_tensor(dist[:, 0, :, tiles], pos[:, :, tiles], low[:, :, tiles], ALU.subtract))
                step(dve.tensor_scalar(dist[:, 1, :, tiles], dist[:, 0, :, tiles], -1.0, None, ALU.add))
                for e in range(2):
                    last = dve.scalar_tensor_tensor(hat[:, e, :, tiles], dist[:, e, :, tiles], -1.0,
                                                    dist[:, e, :, tiles], ALU.mult, ALU.max)
                step(last)
                for e in range(2):
                    last = dve.tensor_scalar(hat[:, e, :, tiles], hat[:, e, :, tiles], 1.0, -1.0, ALU.min, ALU.add)
                step(last)
                for s, (dy, dx) in enumerate(CORNERS):
                    last = dve.tensor_tensor(wgt[:, tiles, s], hat[:, dy, 0, tiles], hat[:, dx, 1, tiles], ALU.mult)
                last.then_inc(wgt_ready, 1)

            for l in range(LAYERS):
                def xt_copy(n):
                    dve.wait_ge(xt_pe, 2 * (l * N + n) + 1)
                    if l:
                        dve.wait_ge(table_out[0][n], 16 * 4)
                    dve.tensor_copy(XT[:, n * TS:n * TS + 4, :], xt_acc[0][:]).then_inc(xt_dve, 1)

                def add_bias(n):
                    dve.wait_ge(off_pe, l * N + n + 1)
                    dve.tensor_tensor(OFT[:, n, :, :], off_acc.rearrange("p (t j) -> p t j", j=NOFF),
                                      rowb[:, l * NOFF:(l + 1) * NOFF].unsqueeze(1).broadcast_to([P, TS, NOFF]),
                                      ALU.add).then_inc(off_ready, 1)

                xt_copy(0)
                dve.wait_ge(setup_cp, SETUPS if l else 1)
                add_bias(0)
                dve.wait_ge(off_ready, l * N + 1)
                positions(0, 1)
                sample_rows(0, 1)
                bilinear_weights(0, 1)
                for n in range(1, AHEAD):
                    xt_copy(n)
                    add_bias(n)
                dve.wait_ge(off_ready, l * N + AHEAD)
                positions(1, AHEAD)
                sample_rows(1, AHEAD)
                dve.wait_ge(wgt_ready, l * N + 1)

                def blend(it, kb):
                    dve.wait_ge(gathered[l][kb % UNITS], it * (16 * GTILES * IBLOCKS // UNITS)
                                + 16 * GTILES * (kb // UNITS + 1))
                    dve.wait_ge(scaled[l], it * IBLOCKS + (kb + 1))
                    v, g = V[:, kb % V_RING, :, :], G[:, kb % UNITS, :, :]
                    for s, to in ((1, v), (2, g[:, :, 3 * C:4 * C])):
                        for r in range(GTILES):
                            last = dve.scalar_tensor_tensor(
                                to[:, r, :], g[:, r, s * C:(s + 1) * C],
                                wgt[:, ds(it * ITILES + (block_tile(kb) + r), 1), s],
                                to[:, r, :], ALU.mult, ALU.add)
                    last.then_inc(corner[l], 1)
                    dve.wait_ge(corner[l], it * IBLOCKS + (kb + 1))
                    dve.tensor_tensor(v, v, g[:, :, 3 * C:4 * C], ALU.add).then_inc(blended[l], 1)

                def image(it, more, jobs=False):
                    for kb in range(IBLOCKS):
                        if more or kb + 1 < IBLOCKS:
                            blend(it, kb + 1)
                        b, g = divmod(kb, GBLOCKS)
                        if kb == GBLOCKS:
                            group_stats(it, 0)
                        if g == 0:
                            dense_hats(it, b)
                        if g in MAKE_S:
                            dense_matrix(it, b, MAKE_S[g])
                        if jobs:
                            if kb in TURN_SUM:
                                xt_copy(TURN_SUM[kb])
                            if kb in OFF_SUM:
                                add_bias(OFF_SUM[kb])
                            if kb == POSITIONS:
                                dve.wait_ge(off_ready, (l + 1) * N)
                                positions(AHEAD, N)
                                sample_rows(AHEAD, N)
                            if kb in WEIGHTS:
                                bilinear_weights(WEIGHTS[kb], WEIGHTS[kb] + 1)
                            if kb == IBLOCKS - 2:
                                dve.wait_ge(wgt_ready, l * N + 2)
                    group_stats(it, 1)

                def dense_hats(it, b):
                    dve.wait_ge(s_ready[l], dense_tile(it, b, 0) + 1)
                    at = pos[:, :, ds(it * ITILES + (b * GT + DENSE_TAP * GTILES), GTILES)]
                    dve.tensor_tensor(dhat[:], at.unsqueeze(3).broadcast_to([P, 2, GTILES, W]),
                                      grid_w[:].unsqueeze(1).unsqueeze(1).broadcast_to([P, 2, GTILES, W]),
                                      ALU.subtract).then_inc(hat_step[l], 1)
                    steps_before = it * (3 * IGROUPS) + 3 * b
                    dve.wait_ge(hat_step[l], steps_before + 1)
                    dve.scalar_tensor_tensor(dhat[:], dhat[:], -1.0, dhat[:], ALU.mult, ALU.max) \
                        .then_inc(hat_step[l], 1)
                    dve.wait_ge(hat_step[l], steps_before + 2)
                    dve.tensor_scalar(dhat[:], dhat[:], 1.0, -1.0, ALU.min, ALU.add).then_inc(hat_step[l], 1)
                    dve.wait_ge(hat_step[l], steps_before + 3)

                def dense_matrix(it, b, j):
                    dve.wait_ge(s_turned[l], dense_tile(it, b, j) + 1)
                    dve.tensor_tensor(S[:, j % 2], dhat[:, 0, j, :].unsqueeze(2).broadcast_to([P, H, W]),
                                      dhat[:, 1, j, :].unsqueeze(1).broadcast_to([P, H, W]),
                                      ALU.mult).then_inc(s_ready[l], 1)

                def group_stats(it, b):
                    dve.wait_ge(acc_cp[l], it * IGROUPS + (b + 1 + 1))
                    dve.bn_stats(stats[:, ds(it * IGROUPS + b, 1), :].rearrange("p g s -> p (g s)"),
                                 A[l][:, ds(it * HW + b * BANK, BANK)]).then_inc(acc_stats[l], 1)

                blend(0, 0)
                image(0, True, jobs=True)
                dve.wait_ge(wgt_ready, (l + 1) * N)
                with dve.Fori(1, N - 1) as it:
                    image(it, True)
                image(N - 1, False)

                dve.wait_ge(acc_stats[l], GROUPS)
                step(dve.bn_aggr(mv[:], stats[:].rearrange("p g s -> p (g s)")))
                dve.tensor_scalar(veps, mv[:, 1:2], BN_EPS, None, ALU.add).then_inc(var_ready, 1)
                dve.wait_ge(small_in, 16 * SMALL)
                dve.wait_ge(root_ready, l + 1)
                dve.wait_ge(var_ready, l + 1)
                step(dve.reciprocal(rinv, root))
                step(dve.tensor_tensor(sq, rinv, rinv, ALU.mult))
                step(dve.tensor_tensor(corr, sq, veps, ALU.mult))
                step(dve.tensor_scalar(corr, corr, -0.5, 1.5, ALU.mult, ALU.add))
                step(dve.tensor_tensor(rinv, rinv, corr, ALU.mult))
                step(dve.tensor_tensor(bn_scale, rinv, bn[l][:, 0:1], ALU.mult))
                step(dve.tensor_tensor(mscale, mv[:, 0:1], bn_scale, ALU.mult))
                dve.tensor_tensor(bn_shift, bn[l][:, 1:2], mscale, ALU.subtract).then_inc(norm_ready, 1)

            dve.wait_ge(norm_ready, LAYERS)
            dve.wait_ge(acc_cp[1], GROUPS + 1)

            def add_residual(n):
                for half in range(2):
                    own = slice(n * HW + half * BANK, n * HW + (half + 1) * BANK)
                    dve.scalar_tensor_tensor(F[:, own], F[:, own], bn_scale, X[:, own], ALU.mult,
                                             ALU.add).then_inc(res_add, 1)

            def take_high(n, j):
                dve.wait_ge(part_cast, 4 * n + j + 1)
                dve.scalar_tensor_tensor(resid[:, j, :], parts[:, j, :], cols[:, 2 + j:3 + j], qk32[:, j, :],
                                         ALU.mult, ALU.add).then_inc(resid_ready, 1)

            def take_middle(n, j):
                dve.wait_ge(part_cast, 4 * n + 2 + j + 1)
                dve.scalar_tensor_tensor(stacks[0:STACK, n, j, :], parts[:, j, :], cols[:, 4 + j:5 + j],
                                         resid[:, j, :], ALU.mult, ALU.add).then_inc(stack_ready, 1)

            def key_max(n, t):
                dve.wait_ge(keymax_full, n * (TS + 1) + t + 1)
                dve.tensor_reduce(nmax[:, n, t:t + 1], keymax_pair(n, t)[:], axis=AX.X, op=ALU.max,
                                  negate=True).then_inc(keymax_free, 1)

            def split_max(n):
                dve.wait_ge(keymax_free, n * TS + TS)
                b = n % 2
                step(dve.tensor_copy(nmax_p[:, b, 0, :], nmax[:, n, :]))
                step(dve.tensor_tensor(nmax_r[:, b, :], nmax[:, n, :], nmax_p[:, b, 0, :], ALU.subtract))
                step(dve.tensor_copy(nmax_p[:, b, 1, :], nmax_r[:, b, :]))
                dve.tensor_tensor(nmax_p[:, b, 2, :], nmax_r[:, b, :], nmax_p[:, b, 1, :],
                                  ALU.subtract).then_inc(max_split, 1)

            def normalise(n):
                dve.wait_ge(weighed, (n + 1) * TS)
                if n:
                    dve.wait_ge(misc_full, JOB["y", n - 1, 1] + 1)
                for t in range(0, TS, 3):
                    tiles = min(3, TS - t)
                    sums = out_acc[t // 3][:, 0:tiles * (C + 1)].rearrange("p (t c) -> p t c", c=C + 1)[:, :, C]
                    dve.reciprocal(einv[:, n, t:t + tiles], sums).then_inc(einv_ready, 1)
                dve.wait_ge(einv_ready, 3 * (n + 1))
                for t in range(YD):
                    dve.tensor_scalar(yT[:, t, :], out_tile(t)[:, 0:C], einv[:, n, t:t + 1], None,
                                      ALU.mult).then_inc(y_ready, 1)

            def misc_copy(job):
                what, n, half = job
                if what == "v":
                    dve.wait_ge(misc_full, JOB[job] + 1)
                    dve.tensor_tensor(vT[:, n, 4 * half:4 * half + 4, 0:C],
                                      job_bank(job).rearrange("p (t c) -> p t c", c=C),
                                      rowb[:, BV:BV + C].unsqueeze(1).broadcast_to([P, 4, C]),
                                      ALU.add).then_inc(misc_free if n else first_v, 1)
                if what == "y":
                    dve.wait_ge(misc_full, JOB[job] + 1)
                    if n:
                        dve.wait_ge(out_dma[half], 16 * n)
                    dve.scalar_tensor_tensor(OUT[:, half, :], job_bank(job), rowb[:, GAM:GAM + 1],
                                             F[:, n * HW + half * BANK:n * HW + (half + 1) * BANK],
                                             ALU.mult, ALU.add).then_inc(out_ready, 1)
                    dve.wait_ge(out_ready, 2 * n + half + 1)
                    dve.sem_inc(misc_free, 1)

            add_residual(0)
            take_high(0, 0)
            take_high(0, 1)
            add_residual(1)
            take_middle(0, 0)
            take_middle(0, 1)
            for s in SLOTS:
                for at in range(TS):
                    if s >= 1 and at == 0:
                        normalise(s - 1)
                    if s + 1 < N:
                        for t in slot_max(s, at):
                            key_max(s + 1, t)
                        if at == split_step(s):
                            split_max(s + 1)
                            if s < 0:
                                for job in FIRST_JOBS:
                                    misc_copy(job)
                    for job in misc_jobs(s, at):
                        misc_copy(job)
                    if s + 2 < N:
                        high_from, middle_from = (3, 5) if s < 0 else (2, 4)
                        if at in (high_from, high_from + 1):
                            take_high(s + 2, at - high_from)
                        if at in (middle_from, middle_from + 1):
                            take_middle(s + 2, at - middle_from)
                    if s + 3 < N and at == (3 if s < 0 else 4):
                        add_residual(s + 3)
            normalise(N - 1)
            for job in LAST_JOBS:
                misc_copy(job)

        @block.tensor
        def _(pe):
            def transposes(bank_cols, tiles):
                for j, tile in enumerate(tiles):
                    last = pe.transpose(bank_cols[:, j * P:(j + 1) * P], tile, ident)
                return last

            def warm_up(count, to=bank[0]):
                for _ in range(count):
                    pe.matmul(to, zeros[:, 0:P], zeros[:], start=True, stop=True)

            pe.wait_ge(consts_dve, 1)
            warm_up(3)
            pe.wait_ge(consts, CONSTS)
            for l in range(LAYERS):
                def turn_input(n, half):
                    if l * N + n:
                        pe.wait_ge((xt_dve, xt_act)[half], l * N + n)
                    if l and n == 0:
                        pe.wait_ge(st_ready[0], N * DTILES + 1)
                    transposes(xt_acc[half], [tile_cols(l, n, 4 * half + j) for j in range(4)]).then_inc(xt_pe, 1)

                def image_in(n):
                    if l == 0:
                        pe.wait_ge(x_in[n], 16)
                    else:
                        pe.wait_ge(xn_ready, n + 1)

                def products(n, half):
                    if half == 0:
                        image_in(n)
                        if l * N + n:
                            pe.wait_ge(z_act, l * N + n)
                    for t in range(4 * half, 4 * half + 4):
                        last = pe.matmul(z_acc[:, t * TAPS * NOFF:(t + 1) * TAPS * NOFF], tile_cols(l, n, t),
                                         off_T[l][:], start=True, stop=True)
                    if half:
                        last.then_inc(z_pe, 1)

                def sum_x(n):
                    pe.wait_ge(z_act, l * N + n + 1)
                    if l * N + n:
                        pe.wait_ge(off_ready, l * N + n)
                    for j in range(KH):
                        last = pe.matmul(u_acc, band[:, j, REACH:REACH + P], ZS[:, j, :, :].rearrange("p t j -> p (t j)"),
                                         start=(j == 0), stop=(j == KH - 1))
                    last.then_inc(u_pe, 1)

                def sum_y(n):
                    pe.wait_ge(u_act, l * N + n + 1)
                    moves = [(0, 0, 0), (-1, -W, 0), (1, W, 0), (-1, P - W, -1), (1, W - P, 1)]
                    for j, (dy, by, other) in enumerate(moves):
                        t0, t1 = max(0, -other), TS - max(0, other)
                        last = pe.matmul(off_acc.rearrange("p (t j) -> p t j", j=NOFF)[:, t0:t1, :],
                                         band[:, 1, REACH + by:REACH + by + P], US[:, t0 + other:t1 + other, dy + 1, :],
                                         start=(j == 0), stop=(j == len(moves) - 1))
                    last.then_inc(off_pe, 1)

                def setup(i):
                    if i:
                        pe.wait_ge(setup_cp, i)
                    if i == 4:
                        pe.wait_ge(off_ready, N)
                    if i in (0, SETUPS - 1):
                        m = min(i, 1)
                        pe.wait_ge(offw_in[m], 16 * 2)
                        w = off_nat[m][:].rearrange("o (c y x) -> o x y c", x=KH, y=KH)
                        for k in range(TAPS):
                            pe.transpose(setup_acc(i)[:, k * NOFF:(k + 1) * NOFF], w[:, k // KH, k % KH, :],
                                         ident[0:NOFF, 0:NOFF])
                    if i == 0:
                        pe.wait_ge(bias_in, 16 * 2)
                        pe.wait_ge(consts_dve, 2)
                        last = pe.matmul(setup_acc(i)[:, 128:128 + NOFF], ones[:], row[:, 0:NOFF], start=True, stop=True)
                    elif i < SETUPS - 1:
                        m, third = divmod(i - 1, 3)
                        pe.wait_ge(dcnw_in[m], 16)
                        w = dcn_nat[m][:].rearrange("o (c k) -> o k c", k=TAPS)
                        last = transposes(setup_acc(i), [w[:, k, :] for k in range(*(0, 4, 8, 9)[third:third + 2])])
                    else:
                        pe.wait_ge(small_in, 16 * SMALL)
                        pe.wait_ge(consts_dve, 2 + MASKS)
                        for j in range(6):
                            pe.matmul(setup_acc(i)[0:STACK, 60 + j:61 + j], cols_row[:, j, :], ones[:, 0:1],
                                      start=True, stop=True)
                        pe.matmul(setup_acc(i)[:, 128:128 + ROWLEN - NOFF], ones[:], row[:, NOFF:ROWLEN],
                                  start=True, stop=True)
                        pe.transpose(setup_acc(i)[:, 320:320 + D], qkv_nat[0:D, 0, :], ident[0:D, 0:D])
                        pe.transpose(setup_acc(i)[:, 352:352 + D], qkv_nat[0:D, 1, :], ident[0:D, 0:D])
                        last = pe.transpose(setup_acc(i)[:, 384:512], qkv_nat[:, 2, :], ident)
                    last.then_inc(setup_pe, 1)

                if l == 0:
                    image_in(0)
                    turn_input(0, 0)
                    turn_input(0, 1)
                    setup(0)
                    pe.wait_ge(setup_cp, 1)
                    products(0, 0)
                    products(0, 1)
                    sum_x(0)
                    sum_y(0)
                    for i in range(1, 4):
                        setup(i)
                else:
                    image_in(0)
                    turn_input(0, 0)
                    turn_input(0, 1)
                    products(0, 0)
                    products(0, 1)
                    sum_x(0)
                    sum_y(0)
                for n in range(1, AHEAD):
                    image_in(n)
                    turn_input(n, 0)
                    turn_input(n, 1)
                    products(n, 0)
                    products(n, 1)
                    sum_x(n)
                    sum_y(n)

                def turn(it, kb):
                    pe.wait_ge(blended[l], it * IBLOCKS + (kb + 1 + G_CREDIT))
                    pe.wait_ge(turned_cp[l], it * IBLOCKS + (kb + 1))
                    transposes(bank[kb % 2], [V[:, kb % V_RING, r, :] for r in range(GTILES)]).then_inc(turned[l], 1)

                def turn_dense(it, b, j):
                    d = dense_tile(it, b, j)
                    pe.wait_ge(s_ready[l], d + 2)
                    pe.wait_ge(st_ready[l], d + 1)
                    rows = P // W
                    transposes(pair[2], [S[:, j % 2, t * rows:(t + 1) * rows, :].rearrange("p h w -> p (h w)")
                                         for t in range(TS)]).then_inc(s_turned[l], 1)

                def use_dense(it, b, j):
                    pe.wait_ge(xs_ready[l], it + 1)
                    pe.wait_ge(st_ready[l], dense_tile(it, b, j) + 2)
                    for t in range(TS):
                        last = pe.matmul(dense_acc[:, j * P:(j + 1) * P], XS[:, t, :],
                                         ST[:, j % 2, t * P:(t + 1) * P], start=(t == 0), stop=(t == TS - 1))
                    last.then_inc(dense_mm[l], 1)

                def image(it, more, jobs=False):
                    for kb in range(IBLOCKS):
                        if jobs:
                            if kb in OFF_SUM:
                                sum_y(OFF_SUM[kb])
                            if kb in Z_FIRST:
                                products(Z_FIRST[kb], 0)
                            if kb in Z_SECOND:
                                products(Z_SECOND[kb], 1)
                            if kb in TURN_SUM:
                                pe.wait_ge(st_ready[l], dense_turned(kb) + 1)
                                turn_input(TURN_SUM[kb], 0)
                                turn_input(TURN_SUM[kb], 1)
                                sum_x(TURN_SUM[kb])
                            if l == 0 and kb in LATE_SETUP:
                                setup(LATE_SETUP[kb])
                        b, g = divmod(kb, GBLOCKS)
                        if g in USE_S:
                            use_dense(it, b, USE_S[g])
                        if g in TURN_S:
                            if jobs:
                                pe.wait_ge(xt_dve, l * N + images_turned(kb))
                                pe.wait_ge(xt_act, l * N + images_turned(kb))
                            turn_dense(it, b, TURN_S[g])
                        turn_next = more or kb + 1 < IBLOCKS
                        if turn_next and g < GBLOCKS - 1:
                            turn(it, kb + 1)
                        if g == 0:
                            pe.wait_ge(acc_cp[l], it * IGROUPS + (b + 1))
                        if g == GBLOCKS - 1:
                            pe.wait_ge(dense_cp[l], it * IGROUPS + (b + 1))
                            pe.matmul(conv_acc, dcn_T[l][:, DENSE_TAP, :], CTD[:], start=False, stop=False)
                        pe.wait_ge(turned_cp[l], it * IBLOCKS + (kb + 1 + CREDIT))
                        pe.matmul(conv_acc, dcn_T[l][:, GATHER_TAPS[g], :], CT[:, kb % 2, :], start=(g == 0),
                                  stop=(g == GBLOCKS - 1)).then_inc(conv_mm[l], 1)
                        if turn_next and g == GBLOCKS - 1:
                            turn(it, kb + 1)

                turn(0, 0)
                if l == 0:
                    pe.wait_ge(setup_cp, 4)
                image(0, True, jobs=True)
                with pe.Fori(1, N - 1) as it:
                    image(it, True)
                image(N - 1, False)
                warm_up(6)

            pe.wait_ge(turned_cp[1], CREDIT + GROUPS * GBLOCKS)
            pe.wait_ge(acc_cp[1], GROUPS + 1)
            pe.wait_ge(identb_ready, 1)

            def misc_job(job):
                what, n, half = job
                to = job_bank(job)
                if misc_uses(job) > 0:
                    pe.wait_ge(misc_free, misc_uses(job))
                if what in "qk":
                    pe.wait_ge(f_ready, 2 * n + half + 1)
                    last = pe.matmul(to[0:STACK], qk_T[:, "qk".index(what), :],
                                     F[:, n * HW + half * BANK:n * HW + (half + 1) * BANK], start=True, stop=True)
                elif what == "v":
                    for j in range(4):
                        at = n * HW + (4 * half + j) * P
                        last = pe.matmul(to[:, j * P:(j + 1) * P], F[:, at:at + P], wv_T[:], start=True, stop=True)
                else:
                    pe.wait_ge(y_ready, n * YD + min(4 * half + 4, YD))
                    if half:
                        pe.wait_ge(y_act, (n + 1) * (TS - YD))
                    last = transposes(to, [yT[:, 4 * half + j, :] for j in range(4)])
                last.then_inc(misc_full, 1)

            def key_scores(n, t):
                use = n * (TS + 1) + t
                if t == 0:
                    pe.wait_ge(stack_ready, 2 * n + 2)
                    if n:
                        pe.wait_ge(stack_full, n)
                elif n:
                    pe.wait_ge(keymax_free, n * TS + t)
                elif t > 1:
                    pe.wait_ge(keymax_free, t - 1)
                for half in range(2):
                    last = pe.matmul(keymax_pair(n, t)[:, half * BANK:(half + 1) * BANK],
                                     stacks[0:STACK, n, 1, t * P:(t + 1) * P],
                                     stacks[0:STACK, n, 0, half * BANK:(half + 1) * BANK], start=True, stop=True)
                last.then_inc(keymax_full, 1)

            def max_rows(n):
                pe.wait_ge(max_split, n + 1)
                for t in range(TS):
                    last = pe.matmul(pair[0][STACK:KROWS, t * P:(t + 1) * P], nmax_p[:, n % 2, :, t], identb[:],
                                     start=True, stop=True)
                last.then_inc(keymax_full, 1)

            def scores(n, j):
                i = n * TS + j
                if j == 0:
                    pe.wait_ge(stack_full, n + 1)
                    pe.wait_ge(ones_ready, 2)
                if i:
                    pe.wait_ge(expd, i)
                for half in range(2):
                    last = pe.matmul(pair[1][:, half * BANK:(half + 1) * BANK],
                                     stacks[0:KROWS, n, 0, j * P:(j + 1) * P],
                                     stacks[0:KROWS, n, 1, half * BANK:(half + 1) * BANK], start=True, stop=True)
                last.then_inc(score_full, 1)

            def weigh(n, j, half):
                pe.wait_ge(expd, n * TS + j + 1)
                if n == 0 and j == 0:
                    pe.wait_ge(first_v, 2)
                    pe.wait_ge(misc_free, 3)
                for t in range(half * 4, half * 4 + 4):
                    if n and j == 0:
                        if t < YD:
                            pe.wait_ge(y_ready, (n - 1) * YD + (t // 3 + 1) * 3)
                        else:
                            pe.wait_ge(y_act, n * (TS - YD))
                    last = pe.matmul(out_acc[t // 3][:, (t % 3) * (C + 1):(t % 3 + 1) * (C + 1)],
                                     probs[:, (n * TS + j) % PRING, t * P:(t + 1) * P], vT[:, n, j, :],
                                     start=(j == 0 and t % 3 == 0), stop=(j == TS - 1), skip_group_check=True)
                if half:
                    last.then_inc(weighed, 1)

            for job in FIRST_JOBS:
                misc_job(job)
            warm_up(3, misc[:])
            for s in SLOTS:
                for step in range(TS):
                    first, *late = (slot_max(s, step) if s + 1 < N else ()) or (None,)
                    jobs = list(misc_jobs(s, step))
                    if s >= 0 and step + 1 < TS:
                        scores(s, step + 1)
                    if s >= 0:
                        if step == 0 and jobs:
                            misc_job(jobs.pop(0))
                        weigh(s, step, 0)
                    if s + 1 < N and step == next_scores(s):
                        scores(s + 1, 0)
                    if first is not None:
                        key_scores(s + 1, first)
                    if s >= 0:
                        weigh(s, step, 1)
                    if s + 1 < N and step == split_step(s) + 1:
                        max_rows(s + 1)
                    for t in late:
                        key_scores(s + 1, t)
                    for job in jobs:
                        misc_job(job)
            for job in LAST_JOBS:
                misc_job(job)


_LAYER = ['tm{}_w', 'tm{}_b', 'tr{}_w', 'tr{}_b', 'dcn{}_w', 'bn{}_g', 'bn{}_b']
_ATTN = ['wq', 'bq', 'wk', 'bk', 'wv', 'bv', 'gamma']


def kernel(**inputs):
    import numpy as _np
    import concourse.bacc as _bacc
    from concourse import mybir as _mybir
    from concourse.bass_utils import run_bass_kernel_spmd as _run

    nc = _bacc.Bacc("TRN2", target_bir_lowering=False, num_devices=1)
    arrays = {}

    def dram(name):
        a = _np.ascontiguousarray(inputs[name])
        if a.ndim == 0:
            a = a.reshape(1)
        arrays[f"in_{name}_dram"] = a
        return nc.dram_tensor(f"in_{name}_dram", a.shape, _mybir.dt.from_np(a.dtype), kind="ExternalInput").ap()

    x = dram("x")
    layers = [[dram("L0_conv_" + name.format(l)) for l in (1, 2)] for name in _LAYER]
    attn = [dram("L1_conv_" + name) for name in _ATTN]
    n, c, h, w = inputs["x"].shape
    out = nc.dram_tensor("out_0_dram", (n, c, h, w), _mybir.dt.float32, kind="ExternalOutput").ap()
    tables = [nc.dram_tensor(f"table{i}", [images * h * w + w + 1, 4 * c], _mybir.dt.float32)
              for i, images in enumerate((1, n - 1))]
    deform_resblock_attention(nc, x, *layers, *attn, out, tables)
    r = _run(nc, [arrays], core_ids=[0])
    return r.results[0]["out_0_dram"]
```
